# Optimizing a Trainium2 kernel written in Bass

```python
import numpy as np
import jax
import jax.numpy as jnp

def _softmax(x, axis=-1):
    return jax.nn.softmax(x, axis=axis)

def _gelu(x):
    return jax.nn.gelu(x, approximate=True)

def _silu(x):
    return jax.nn.silu(x)

def _sigmoid(x):
    return jax.nn.sigmoid(x)

def _layernorm(x, axis=-1, eps=1e-05):
    m = jnp.mean(x, axis=axis, keepdims=True)
    v = jnp.var(x, axis=axis, keepdims=True)
    return (x - m) / jnp.sqrt(v + eps)

def _scatter_add(tgt, idx, src, axis=0):
    return tgt.at[idx].add(src)

def _segment_sum(src, seg, n):
    return jax.ops.segment_sum(src, seg, n)
kernel_name = 'mk_xattn_ffn_d4_seqx_r8_8577d0'

def setup_inputs(seed: int=0):
    np.random.seed(seed)
    _w = jnp.asarray

    def _rec_inputs():
        import jax
        import jax.numpy as jnp
        _rk = jax.random.key(seed)
        x = 7.22e-05 + 1 * jax.random.normal(jax.random.fold_in(_rk, 1), (8, 128, 256), jnp.float32)
        _lenS = 128 - jax.random.randint(jax.random.fold_in(_rk, 7), (8,), 0, max(1, 128 // 4) + 1, jnp.int32)
        _lenS2 = 128 - jax.random.randint(jax.random.fold_in(_rk, 8), (8,), 0, max(1, 128 // 4) + 1, jnp.int32)
        _ctx_2048P = jax.random.normal(jax.random.fold_in(_rk, 11), (8, 16, 256), jnp.float32)
        _ctx_2048c = jax.random.dirichlet(jax.random.fold_in(_rk, 511), 0.3 * jnp.ones((16,), jnp.float32), (8, 128))
        _ctx_2048t = jnp.einsum('bsk,bkd->bsd', _ctx_2048c, _ctx_2048P)
        _ctx_2048t = _ctx_2048t * jax.lax.rsqrt(jnp.mean(jnp.square(_ctx_2048t)) + 1e-12) * 0.953939
        ctx_2048 = 4.13588e-05 + 0.999923 * (_ctx_2048t + 0.3 * jax.random.normal(jax.random.fold_in(_rk, 611), (8, 128, 256), jnp.float32))
        _validS = jnp.arange(128)[None, :] < _lenS[:, None]
        _validS2 = jnp.arange(128)[None, :] < _lenS2[:, None]
        _causal = jnp.tril(jnp.ones((128, 128), dtype=bool))
        mask_Bx1x2048_fk1 = jnp.where(jnp.ones((8, 1, 256), dtype=bool), 1.0, 0.0).astype(jnp.float32)
        mask_BxS2_ik0 = jnp.where(jnp.broadcast_to(_validS2[:, :], (8, 128)), 0, 1).astype(jnp.int32)
        return (x, ctx_2048, mask_Bx1x2048_fk1, mask_BxS2_ik0)
    x, ctx_2048, mask_Bx1x2048_fk1, mask_BxS2_ik0 = _rec_inputs()

    def _L0_xattn_setup():
        import jax, jax.numpy as jnp
        import numpy as np
        B, S, DIM, HD = (4, 128, 256, 128)
        H = DIM // HD
        GN_EPS = 0.001

        def _decay_masks(n_heads, seq_len):
            gam = 1.0 - 2.0 ** (-5.0 - jnp.arange(n_heads, dtype=jnp.float32))
            idx = jnp.arange(seq_len, dtype=jnp.float32)
            expo = idx[None, :] - idx[:, None]
            D = jnp.where(expo[None, :, :] <= 0, gam[:, None, None] ** expo[None, :, :], 0.0)
            return D / jnp.sqrt(D.sum(axis=-1))[:, None, :]
        key = jax.random.key(seed)
        ks = jax.random.split(key, 8)
        x = jax.random.normal(ks[0], (B, S, DIM), dtype=jnp.float32)
        k = jax.random.normal(ks[1], (B, S, DIM), dtype=jnp.float32)
        v = jax.random.normal(ks[2], (B, S, DIM), dtype=jnp.float32)
        Wh = jax.random.normal(ks[3], (H, HD, HD), dtype=jnp.float32) / np.sqrt(HD)
        wg_w = jax.random.normal(ks[4], (DIM, DIM), dtype=jnp.float32) / np.sqrt(DIM)
        wo_w = jax.random.normal(ks[5], (DIM, DIM), dtype=jnp.float32) / np.sqrt(DIM)
        gn_gamma = jnp.ones((DIM,), dtype=jnp.float32)
        gn_beta = jnp.zeros((DIM,), dtype=jnp.float32)
        return {'x': x, 'k': k, 'v': v, 'Wh': Wh, 'wg_w': wg_w, 'wo_w': wo_w, 'gn_gamma': gn_gamma, 'gn_beta': gn_beta}
    _L0_xattn_all = _L0_xattn_setup()
    _L0_xattn_in = {k: v for k, v in _L0_xattn_all.items() if k in ('Wh', 'wg_w', 'wo_w', 'gn_gamma', 'gn_beta')}
    del _L0_xattn_all

    def _L0_ffn_setup():
        import jax, jax.numpy as jnp
        import numpy as np
        FP8_MAX = 448.0

        def _fp8_matmul(x2d, w):
            scale_x = jnp.maximum(jnp.max(jnp.abs(x2d)) / FP8_MAX, 1e-06)
            scale_w = jnp.maximum(jnp.max(jnp.abs(w)) / FP8_MAX, 1e-06)
            x8 = (x2d / scale_x).astype(jnp.float8_e4m3fn)
            w8 = (w / scale_w).astype(jnp.float8_e4m3fn)
            out = jnp.matmul(x8.astype(x2d.dtype), w8.astype(x2d.dtype).T)
            return out * (scale_x * scale_w)
        key = jax.random.key(seed)
        k1, k2, k3 = jax.random.split(key, 3)
        dim = 256
        B, S = (4, 256)
        x = jax.random.normal(k1, (B, S, dim), dtype=jnp.float32)
        std = 0.5 * dim ** (-0.5)
        w_fc = jax.random.normal(k2, (4 * dim, dim), dtype=jnp.float32) * std
        w_proj = jax.random.normal(k3, (dim, 4 * dim), dtype=jnp.float32) * std
        return {'x': x, 'w_fc': w_fc, 'w_proj': w_proj}
    _L0_ffn_all = _L0_ffn_setup()
    _L0_ffn_in = {k: v for k, v in _L0_ffn_all.items() if k in ('w_fc', 'w_proj')}
    del _L0_ffn_all

    def _L1_xattn_setup():
        import math
        import jax, jax.numpy as jnp
        import numpy as np
        SIZE = 128
        HEADS = 16
        HEAD_DIM = SIZE // HEADS
        B, T, S = (2, 256, 256)
        NEG = 1000000.0
        key = jax.random.key(seed)
        ks = jax.random.split(key, 10)
        target = jax.random.normal(ks[0], (B, SIZE, T), dtype=jnp.float32)
        source = jax.random.normal(ks[1], (B, SIZE, S), dtype=jnp.float32)
        target_mask = (jax.random.uniform(ks[2], (B, 1, T)) > 0.1).astype(jnp.float32)
        source_mask = (jax.random.uniform(ks[3], (B, 1, S)) > 0.1).astype(jnp.float32)
        scale = 1.0 / math.sqrt(SIZE)
        Wq = jax.random.normal(ks[4], (SIZE, SIZE), dtype=jnp.float32) * scale
        Wk = jax.random.normal(ks[5], (SIZE, SIZE), dtype=jnp.float32) * scale
        Wv = jax.random.normal(ks[6], (SIZE, SIZE), dtype=jnp.float32) * scale
        bq = jax.random.normal(ks[7], (SIZE,), dtype=jnp.float32) * 0.01
        bk = jax.random.normal(ks[8], (SIZE,), dtype=jnp.float32) * 0.01
        bv = jax.random.normal(ks[9], (SIZE,), dtype=jnp.float32) * 0.01
        return {'target': target, 'source': source, 'target_mask': target_mask, 'source_mask': source_mask, 'Wq': Wq, 'bq': bq, 'Wk': Wk, 'bk': bk, 'Wv': Wv, 'bv': bv}
    _L1_xattn_all = _L1_xattn_setup()
    _L1_xattn_in = {k: v for k, v in _L1_xattn_all.items() if k in ('Wq', 'bq', 'Wk', 'bk', 'Wv', 'bv')}
    del _L1_xattn_all

    def _L1_ffn_setup():
        import jax, jax.numpy as jnp
        import numpy as np
        LORA_ALPHA = 16.0
        TOP_K = 2
        key = jax.random.key(seed)
        k_x, k_w, k_g, k_a, k_b = jax.random.split(key, 5)
        B, S, H, O, E, R = (2, 256, 256, 256, 8, 16)
        x = jax.random.normal(k_x, (B, S, H), dtype=jnp.float32)
        weight = jax.random.normal(k_w, (O, H), dtype=jnp.float32)
        gate_w = jax.random.normal(k_g, (E, H), dtype=jnp.float32) * 0.02
        A_w = jax.random.normal(k_a, (E, R, H), dtype=jnp.float32) * (1.0 / np.sqrt(H))
        B_w = jax.random.normal(k_b, (E, O, R), dtype=jnp.float32) * 0.01
        return {'x': x, 'weight': weight, 'gate_w': gate_w, 'A_w': A_w, 'B_w': B_w}
    _L1_ffn_all = _L1_ffn_setup()
    _L1_ffn_in = {k: v for k, v in _L1_ffn_all.items() if k in ('weight', 'gate_w', 'A_w', 'B_w')}
    del _L1_ffn_all

    def _L2_xattn_setup():
        import jax, jax.numpy as jnp
        import numpy as np
        DIM = 256
        NHEADS = 32
        HEAD_DIM = DIM // NHEADS
        EPS = 1e-06

        def _rmsnorm(t):
            return t * jax.lax.rsqrt(jnp.mean(t * t, axis=-1, keepdims=True) + EPS)
        key = jax.random.key(seed)
        kx, kc, kq, kk, kv = jax.random.split(key, 5)
        x = jax.random.normal(kx, (2, 512, DIM), dtype=jnp.float32)
        context = jax.random.normal(kc, (2, 64, DIM), dtype=jnp.float32)
        std = 0.02
        Wq = jax.random.normal(kq, (DIM, DIM), dtype=jnp.float32) * std
        Wk = jax.random.normal(kk, (DIM, DIM), dtype=jnp.float32) * std
        Wv = jax.random.normal(kv, (DIM, DIM), dtype=jnp.float32) * std
        return {'x': x, 'context': context, 'Wq': Wq, 'Wk': Wk, 'Wv': Wv}
    _L2_xattn_all = _L2_xattn_setup()
    _L2_xattn_in = {k: v for k, v in _L2_xattn_all.items() if k in ('Wq', 'Wk', 'Wv')}
    del _L2_xattn_all

    def _L2_ffn_setup():
        import jax, jax.numpy as jnp
        import numpy as np
        E, TOPK, H, I, NSH = (8, 2, 256, 640, 2)
        B, S = (2, 128)
        key = jax.random.key(seed)
        ks = jax.random.split(key, 8)
        sc = 0.02
        return {'x': jax.random.normal(ks[0], (B, S, H), dtype=jnp.float32), 'w_router': jax.random.normal(ks[1], (E, H), dtype=jnp.float32), 'wg': jax.random.normal(ks[2], (E, I, H), dtype=jnp.float32) * sc, 'wu': jax.random.normal(ks[3], (E, I, H), dtype=jnp.float32) * sc, 'wd': jax.random.normal(ks[4], (E, H, I), dtype=jnp.float32) * sc, 'sg': jax.random.normal(ks[5], (NSH, I, H), dtype=jnp.float32) * sc, 'su': jax.random.normal(ks[6], (NSH, I, H), dtype=jnp.float32) * sc, 'sd': jax.random.normal(ks[7], (NSH, H, I), dtype=jnp.float32) * sc}
    _L2_ffn_all = _L2_ffn_setup()
    _L2_ffn_in = {k: v for k, v in _L2_ffn_all.items() if k in ('w_router', 'wg', 'wu', 'wd', 'sg', 'su', 'sd')}
    del _L2_ffn_all

    def _L3_xattn_setup():
        import jax, jax.numpy as jnp
        import numpy as np
        import math
        H = 256
        NH = 16
        HD = H // NH
        EPS_LN = 1e-05
        RES_SCALE_MAX = 0.3

        def _nan_clean(x, lim=10000.0):
            return jnp.nan_to_num(x, nan=0.0, posinf=lim, neginf=-lim)
        key = jax.random.key(seed)
        ks = jax.random.split(key, 12)
        B, S, T = (4, 256, 32)
        std = 1.0 / math.sqrt(H)
        return {'hidden_states': jax.random.normal(ks[0], (B, S, H), jnp.float32), 'audio_tokens': jax.random.normal(ks[1], (B, T, H), jnp.float32), 'attention_mask': jax.random.randint(ks[2], (B, T), 0, 2, jnp.int32), 'Wq': jax.random.normal(ks[3], (H, H), jnp.float32) * std, 'bq': jnp.zeros((H,), jnp.float32), 'Wk': jax.random.normal(ks[4], (H, H), jnp.float32) * std, 'bk': jnp.zeros((H,), jnp.float32), 'Wv': jax.random.normal(ks[5], (H, H), jnp.float32) * std, 'bv': jnp.zeros((H,), jnp.float32), 'Wo': jax.random.normal(ks[6], (H, H), jnp.float32) * std, 'bo': jnp.zeros((H,), jnp.float32), 'ln_gamma': jnp.ones((H,), jnp.float32), 'ln_beta': jnp.zeros((H,), jnp.float32), 'residual_scale': jnp.float32(0.05)}
    _L3_xattn_all = _L3_xattn_setup()
    _L3_xattn_in = {k: v for k, v in _L3_xattn_all.items() if k in ('Wq', 'bq', 'Wk', 'bk', 'Wv', 'bv', 'Wo', 'bo', 'ln_gamma', 'ln_beta', 'residual_scale')}
    del _L3_xattn_all

    def _L3_ffn_setup():
        import jax, jax.numpy as jnp
        import numpy as np
        B, L, D = (2, 128, 256)
        E, K = (8, 2)
        H, HS = (176, 352)
        key = jax.random.key(seed)
        ks = jax.random.split(key, 9)
        s = 0.02
        return {'x': jax.random.normal(ks[0], (B, L, D), dtype=jnp.float32), 'gate_w': jax.random.normal(ks[1], (E, D), dtype=jnp.float32) * s, 'w_gate': jax.random.normal(ks[2], (E, D, H), dtype=jnp.float32) * s, 'w_up': jax.random.normal(ks[3], (E, D, H), dtype=jnp.float32) * s, 'w_down': jax.random.normal(ks[4], (E, H, D), dtype=jnp.float32) * s, 'shgate_w': jax.random.normal(ks[5], (D,), dtype=jnp.float32) * s, 'shw_gate': jax.random.normal(ks[6], (D, HS), dtype=jnp.float32) * s, 'shw_up': jax.random.normal(ks[7], (D, HS), dtype=jnp.float32) * s, 'shw_down': jax.random.normal(ks[8], (HS, D), dtype=jnp.float32) * s}
    _L3_ffn_all = _L3_ffn_setup()
    _L3_ffn_in = {k: v for k, v in _L3_ffn_all.items() if k in ('gate_w', 'w_gate', 'w_up', 'w_down', 'shgate_w', 'shw_gate', 'shw_up', 'shw_down')}
    del _L3_ffn_all
    return {'x': x, 'ctx_2048': ctx_2048, 'mask_Bx1x2048_fk1': mask_Bx1x2048_fk1, 'mask_BxS2_ik0': mask_BxS2_ik0, 'L0_xattn_Wh': _L0_xattn_in['Wh'], 'L0_xattn_wg_w': _L0_xattn_in['wg_w'], 'L0_xattn_wo_w': _L0_xattn_in['wo_w'], 'L0_xattn_gn_gamma': _L0_xattn_in['gn_gamma'], 'L0_xattn_gn_beta': _L0_xattn_in['gn_beta'], 'L0_ffn_w_fc': _L0_ffn_in['w_fc'], 'L0_ffn_w_proj': _L0_ffn_in['w_proj'], 'L1_xattn_Wq': _L1_xattn_in['Wq'], 'L1_xattn_bq': _L1_xattn_in['bq'], 'L1_xattn_Wk': _L1_xattn_in['Wk'], 'L1_xattn_bk': _L1_xattn_in['bk'], 'L1_xattn_Wv': _L1_xattn_in['Wv'], 'L1_xattn_bv': _L1_xattn_in['bv'], 'L1_ffn_weight': _L1_ffn_in['weight'], 'L1_ffn_gate_w': _L1_ffn_in['gate_w'], 'L1_ffn_A_w': _L1_ffn_in['A_w'], 'L1_ffn_B_w': _L1_ffn_in['B_w'], 'L2_xattn_Wq': _L2_xattn_in['Wq'], 'L2_xattn_Wk': _L2_xattn_in['Wk'], 'L2_xattn_Wv': _L2_xattn_in['Wv'], 'L2_ffn_w_router': _L2_ffn_in['w_router'], 'L2_ffn_wg': _L2_ffn_in['wg'], 'L2_ffn_wu': _L2_ffn_in['wu'], 'L2_ffn_wd': _L2_ffn_in['wd'], 'L2_ffn_sg': _L2_ffn_in['sg'], 'L2_ffn_su': _L2_ffn_in['su'], 'L2_ffn_sd': _L2_ffn_in['sd'], 'L3_xattn_Wq': _L3_xattn_in['Wq'], 'L3_xattn_bq': _L3_xattn_in['bq'], 'L3_xattn_Wk': _L3_xattn_in['Wk'], 'L3_xattn_bk': _L3_xattn_in['bk'], 'L3_xattn_Wv': _L3_xattn_in['Wv'], 'L3_xattn_bv': _L3_xattn_in['bv'], 'L3_xattn_Wo': _L3_xattn_in['Wo'], 'L3_xattn_bo': _L3_xattn_in['bo'], 'L3_xattn_ln_gamma': _L3_xattn_in['ln_gamma'], 'L3_xattn_ln_beta': _L3_xattn_in['ln_beta'], 'L3_xattn_residual_scale': _L3_xattn_in['residual_scale'], 'L3_ffn_gate_w': _L3_ffn_in['gate_w'], 'L3_ffn_w_gate': _L3_ffn_in['w_gate'], 'L3_ffn_w_up': _L3_ffn_in['w_up'], 'L3_ffn_w_down': _L3_ffn_in['w_down'], 'L3_ffn_shgate_w': _L3_ffn_in['shgate_w'], 'L3_ffn_shw_gate': _L3_ffn_in['shw_gate'], 'L3_ffn_shw_up': _L3_ffn_in['shw_up'], 'L3_ffn_shw_down': _L3_ffn_in['shw_down']}

def reference(x, ctx_2048, mask_Bx1x2048_fk1, mask_BxS2_ik0, L0_xattn_Wh, L0_xattn_wg_w, L0_xattn_wo_w, L0_xattn_gn_gamma, L0_xattn_gn_beta, L0_ffn_w_fc, L0_ffn_w_proj, L1_xattn_Wq, L1_xattn_bq, L1_xattn_Wk, L1_xattn_bk, L1_xattn_Wv, L1_xattn_bv, L1_ffn_weight, L1_ffn_gate_w, L1_ffn_A_w, L1_ffn_B_w, L2_xattn_Wq, L2_xattn_Wk, L2_xattn_Wv, L2_ffn_w_router, L2_ffn_wg, L2_ffn_wu, L2_ffn_wd, L2_ffn_sg, L2_ffn_su, L2_ffn_sd, L3_xattn_Wq, L3_xattn_bq, L3_xattn_Wk, L3_xattn_bk, L3_xattn_Wv, L3_xattn_bv, L3_xattn_Wo, L3_xattn_bo, L3_xattn_ln_gamma, L3_xattn_ln_beta, L3_xattn_residual_scale, L3_ffn_gate_w, L3_ffn_w_gate, L3_ffn_w_up, L3_ffn_w_down, L3_ffn_shgate_w, L3_ffn_shw_gate, L3_ffn_shw_up, L3_ffn_shw_down):
    import jax
    import jax.numpy as jnp

    def _L0_xattn_ref(x, k, v, Wh, wg_w, wo_w, gn_gamma, gn_beta):
        import jax, jax.numpy as jnp
        import numpy as np
        B, S, DIM, HD = (4, 128, 256, 128)
        H = DIM // HD
        GN_EPS = 0.001

        def _decay_masks(n_heads, seq_len):
            gam = 1.0 - 2.0 ** (-5.0 - jnp.arange(n_heads, dtype=jnp.float32))
            idx = jnp.arange(seq_len, dtype=jnp.float32)
            expo = idx[None, :] - idx[:, None]
            D = jnp.where(expo[None, :, :] <= 0, gam[:, None, None] ** expo[None, :, :], 0.0)
            return D / jnp.sqrt(D.sum(axis=-1))[:, None, :]
        b, s, dim = x.shape
        h, hd, _ = Wh.shape
        xh = x.reshape(b, s, h, hd)
        kh = k.reshape(b, s, h, hd)
        vh = v.reshape(b, s, h, hd)
        Q = jnp.einsum('bshd,hde->bshe', xh, Wh)
        K = jnp.einsum('bshd,hde->bshe', kh, Wh)
        V = jnp.einsum('bshd,hde->bshe', vh, Wh)
        scores = jnp.einsum('bshe,bthe->bhst', Q, K) / jnp.sqrt(jnp.float32(hd))
        Dn = _decay_masks(h, s)
        masked = scores * Dn[None, :, :, :]
        A = jnp.maximum(jnp.abs(masked.sum(axis=0)), 1.0)
        O = jnp.einsum('hst,bthe->bshe', A, V).reshape(b, s, dim)
        mu = O.mean(axis=-1, keepdims=True)
        var = O.var(axis=-1, keepdims=True)
        Y = (O - mu) / jnp.sqrt(var + GN_EPS) * gn_gamma + gn_beta
        W = jax.nn.relu(x @ wg_w)
        return W * Y @ wo_w

    def _L0_ffn_ref(x, w_fc, w_proj):
        import jax, jax.numpy as jnp
        import numpy as np
        FP8_MAX = 448.0

        def _fp8_matmul(x2d, w):
            scale_x = jnp.maximum(jnp.max(jnp.abs(x2d)) / FP8_MAX, 1e-06)
            scale_w = jnp.maximum(jnp.max(jnp.abs(w)) / FP8_MAX, 1e-06)
            x8 = (x2d / scale_x).astype(jnp.float8_e4m3fn)
            w8 = (w / scale_w).astype(jnp.float8_e4m3fn)
            out = jnp.matmul(x8.astype(x2d.dtype), w8.astype(x2d.dtype).T)
            return out * (scale_x * scale_w)
        shape = x.shape
        x2d = x.reshape(-1, shape[-1])
        h = _fp8_matmul(x2d, w_fc)
        h = jnp.square(jax.nn.relu(h))
        out = _fp8_matmul(h, w_proj)
        return out.reshape(*shape[:-1], -1)

    def _L1_xattn_ref(target, source, target_mask, source_mask, Wq, bq, Wk, bk, Wv, bv):
        import math
        import jax, jax.numpy as jnp
        import numpy as np
        SIZE = 128
        HEADS = 16
        HEAD_DIM = SIZE // HEADS
        B, T, S = (2, 256, 256)
        NEG = 1000000.0
        b, _, t = target.shape
        s = source.shape[-1]
        q = jnp.einsum('oc,bct->bot', Wq, target) + bq[None, :, None]
        k = jnp.einsum('oc,bcs->bos', Wk, source) + bk[None, :, None]
        v = jnp.einsum('oc,bcs->bos', Wv, source) + bv[None, :, None]
        q = q.reshape(b, HEADS, HEAD_DIM, t)
        k = k.reshape(b, HEADS, HEAD_DIM, s)
        v = v.reshape(b, HEADS, HEAD_DIM, s)
        dot = jnp.einsum('bhdt,bhds->bhts', q, k) / math.sqrt(HEAD_DIM)
        mask = target_mask[:, :, :, None] * source_mask[:, :, None, :]
        dot = mask * dot - (1.0 - mask) * NEG
        amap = jax.nn.softmax(dot, axis=-1) * mask
        out = jnp.einsum('bhts,bhds->bhdt', amap, v)
        return out.reshape(b, HEADS * HEAD_DIM, t)

    def _L1_ffn_ref(x, weight, gate_w, A_w, B_w):
        import jax, jax.numpy as jnp
        import numpy as np
        LORA_ALPHA = 16.0
        TOP_K = 2
        E = gate_w.shape[0]
        out = jnp.einsum('bsh,oh->bso', x, weight)
        logits = jnp.einsum('bsh,eh->bse', x, gate_w)
        probs = jax.nn.softmax(logits, axis=-1)
        topk_w, topk_idx = jax.lax.top_k(probs, TOP_K)
        topk_w = topk_w / jnp.sum(topk_w, axis=-1, keepdims=True)
        onehot = jax.nn.one_hot(topk_idx, E, dtype=x.dtype)
        cw = jnp.einsum('bsk,bske->bse', topk_w, onehot)
        t = jnp.einsum('bsh,erh->bser', x, A_w)
        t = t * cw[..., None]
        lora = jnp.einsum('bser,eor->bso', t, B_w)
        return out + LORA_ALPHA * lora

    def _L2_xattn_ref(x, context, Wq, Wk, Wv):
        import jax, jax.numpy as jnp
        import numpy as np
        DIM = 256
        NHEADS = 32
        HEAD_DIM = DIM // NHEADS
        EPS = 1e-06

        def _rmsnorm(t):
            return t * jax.lax.rsqrt(jnp.mean(t * t, axis=-1, keepdims=True) + EPS)
        b, n, _ = x.shape
        m = context.shape[1]
        q = x @ Wq.T
        k_raw = context @ Wk.T
        v_raw = context @ Wv.T
        q = q.reshape(b, n, NHEADS, HEAD_DIM).transpose(0, 2, 1, 3)
        kv = jnp.concatenate([k_raw, v_raw], axis=-1)
        kv = kv.reshape(b, m, NHEADS, HEAD_DIM, 2)
        k = kv[..., 0].transpose(0, 2, 1, 3)
        v = kv[..., 1].transpose(0, 2, 1, 3)
        q = _rmsnorm(q)
        k = _rmsnorm(k)
        scale = HEAD_DIM ** (-0.5)
        scores = jnp.einsum('bhnd,bhmd->bhnm', q, k) * scale
        attn = jax.nn.softmax(scores, axis=-1)
        out = jnp.einsum('bhnm,bhmd->bhnd', attn, v)
        return out.transpose(0, 2, 1, 3).reshape(b, n, NHEADS * HEAD_DIM)

    def _L2_ffn_ref(x, w_router, wg, wu, wd, sg, su, sd):
        import jax, jax.numpy as jnp
        import numpy as np
        E, TOPK, H, I, NSH = (8, 2, 256, 640, 2)
        B, S = (2, 128)
        b, s, h = x.shape
        xt = x.reshape(-1, h)
        T = xt.shape[0]
        logits = jnp.einsum('th,eh->te', xt.astype(jnp.float32), w_router.astype(jnp.float32))
        scores = jax.nn.sigmoid(logits)
        topk_w, topk_i = jax.lax.top_k(scores, TOPK)
        topk_w = topk_w / jnp.sum(topk_w, axis=-1, keepdims=True)
        comb = jnp.zeros((T, E), dtype=xt.dtype)
        comb = comb.at[jnp.arange(T)[:, None], topk_i].add(topk_w.astype(xt.dtype))
        gate = jax.nn.silu(jnp.einsum('th,eih->tei', xt, wg))
        up = jnp.einsum('th,eih->tei', xt, wu)
        expert_out = jnp.einsum('tei,ehi->teh', gate * up, wd)
        out = jnp.einsum('te,teh->th', comb, expert_out)
        sgate = jax.nn.silu(jnp.einsum('th,jih->tji', xt, sg))
        sup = jnp.einsum('th,jih->tji', xt, su)
        out = out + jnp.einsum('tji,jhi->th', sgate * sup, sd)
        return out.reshape(b, s, h)

    def _L3_xattn_ref(hidden_states, audio_tokens, attention_mask, Wq, bq, Wk, bk, Wv, bv, Wo, bo, ln_gamma, ln_beta, residual_scale):
        import jax, jax.numpy as jnp
        import numpy as np
        import math
        H = 256
        NH = 16
        HD = H // NH
        EPS_LN = 1e-05
        RES_SCALE_MAX = 0.3

        def _nan_clean(x, lim=10000.0):
            return jnp.nan_to_num(x, nan=0.0, posinf=lim, neginf=-lim)
        B, S, _ = hidden_states.shape
        T = audio_tokens.shape[1]
        hs = _nan_clean(hidden_states).astype(jnp.float32)
        at = _nan_clean(audio_tokens).astype(jnp.float32)

        def proj(x, W, b, L):
            y = x @ W.T + b
            return y.reshape(B, L, NH, HD).transpose(0, 2, 1, 3)
        q = _nan_clean(proj(hs, Wq, bq, S))
        k = _nan_clean(proj(at, Wk, bk, T))
        v = _nan_clean(proj(at, Wv, bv, T))
        scale = max(math.sqrt(HD), 1e-08)
        scores = jnp.einsum('bhsd,bhtd->bhst', q, k) / scale
        scores = jnp.clip(scores, -50.0, 50.0)
        scores = jnp.nan_to_num(scores, nan=0.0, posinf=50.0, neginf=-50.0)
        attend = (attention_mask.astype(jnp.float32) > 0.5)[:, None, None, :]
        scores = jnp.where(attend, scores, -10000.0)
        scores = jnp.clip(scores, -50.0, 50.0)
        probs = jax.nn.softmax(scores, axis=-1)
        probs = jnp.nan_to_num(probs, nan=0.0, posinf=1.0, neginf=0.0)
        probs = probs / (probs.sum(axis=-1, keepdims=True) + 1e-08)
        ctx = jnp.einsum('bhst,bhtd->bhsd', probs, v)
        ctx = ctx.transpose(0, 2, 1, 3).reshape(B, S, H)
        delta = _nan_clean(ctx @ Wo.T + bo)
        rs = jnp.clip(residual_scale, 0.0, RES_SCALE_MAX)
        delta = rs * delta
        mu = delta.mean(axis=-1, keepdims=True)
        var = jnp.mean((delta - mu) ** 2, axis=-1, keepdims=True)
        delta = (delta - mu) / jnp.sqrt(var + EPS_LN) * ln_gamma + ln_beta
        return delta

    def _L3_ffn_ref(x, gate_w, w_gate, w_up, w_down, shgate_w, shw_gate, shw_up, shw_down):
        import jax, jax.numpy as jnp
        import numpy as np
        B, L, D = (2, 128, 256)
        E, K = (8, 2)
        H, HS = (176, 352)
        b, l, d = x.shape
        xf = x.reshape(-1, d)
        logits = jnp.einsum('td,ed->te', xf.astype(jnp.float32), gate_w)
        probs = jax.nn.softmax(logits.astype(jnp.float32), axis=-1)
        weights, indices = jax.lax.top_k(probs, K)
        weights = (weights / weights.sum(-1, keepdims=True)).astype(x.dtype)
        onehot = jax.nn.one_hot(indices, E, dtype=x.dtype)
        combine = jnp.einsum('tk,tke->te', weights, onehot)
        g = jnp.einsum('td,edh->teh', xf, w_gate)
        u = jnp.einsum('td,edh->teh', xf, w_up)
        h = jax.nn.silu(g) * u
        out = jnp.einsum('teh,ehd,te->td', h.astype(jnp.float32), w_down.astype(jnp.float32), combine.astype(jnp.float32))
        sgate = jax.nn.sigmoid(xf @ shgate_w)[:, None]
        sh = jax.nn.silu(xf @ shw_gate) * (xf @ shw_up) @ shw_down
        out = out + (sgate * sh).astype(jnp.float32)
        return out.astype(x.dtype).reshape(b, l, d)
    x = x + _L0_xattn_ref(_layernorm(x, axis=-1), ctx_2048, ctx_2048, L0_xattn_Wh, L0_xattn_wg_w, L0_xattn_wo_w, L0_xattn_gn_gamma, L0_xattn_gn_beta)
    x = x + _L0_ffn_ref(_layernorm(x, axis=-1), L0_ffn_w_fc, L0_ffn_w_proj)
    x = x + _L1_xattn_ref(_layernorm(x, axis=-1), ctx_2048, mask_Bx1x2048_fk1, mask_Bx1x2048_fk1, L1_xattn_Wq, L1_xattn_bq, L1_xattn_Wk, L1_xattn_bk, L1_xattn_Wv, L1_xattn_bv)
    x = x + _L1_ffn_ref(_layernorm(x, axis=-1), L1_ffn_weight, L1_ffn_gate_w, L1_ffn_A_w, L1_ffn_B_w)
    x = x + _L2_xattn_ref(_layernorm(x, axis=-1), ctx_2048, L2_xattn_Wq, L2_xattn_Wk, L2_xattn_Wv)
    x = x + _L2_ffn_ref(_layernorm(x, axis=-1), L2_ffn_w_router, L2_ffn_wg, L2_ffn_wu, L2_ffn_wd, L2_ffn_sg, L2_ffn_su, L2_ffn_sd)
    x = x + _L3_xattn_ref(_layernorm(x, axis=-1), ctx_2048, mask_BxS2_ik0, L3_xattn_Wq, L3_xattn_bq, L3_xattn_Wk, L3_xattn_bk, L3_xattn_Wv, L3_xattn_bv, L3_xattn_Wo, L3_xattn_bo, L3_xattn_ln_gamma, L3_xattn_ln_beta, L3_xattn_residual_scale)
    x = x + _L3_ffn_ref(_layernorm(x, axis=-1), L3_ffn_gate_w, L3_ffn_w_gate, L3_ffn_w_up, L3_ffn_w_down, L3_ffn_shgate_w, L3_ffn_shw_gate, L3_ffn_shw_up, L3_ffn_shw_down)
    return x

_drawn_inputs = setup_inputs


def setup_inputs(seed=0):
    import zlib

    import numpy as np

    out = dict(_drawn_inputs(seed))
    spreads = {'L0_xattn_gn_gamma': (1.0, 0.2),
     'L0_xattn_gn_beta': (0.0, 0.1),
     'L3_xattn_bq': (0.0, 2.0),
     'L3_xattn_bk': (0.0, 2.0),
     'L3_xattn_bv': (0.0, 0.8),
     'L3_xattn_bo': (0.0, 0.8),
     'L3_xattn_ln_gamma': (1.0, 0.6),
     'L3_xattn_ln_beta': (0.0, 0.8)}
    factors = {'L1_xattn_bq': 8.0,
     'L1_xattn_bk': 200.0,
     'L1_xattn_bv': 175.82,
     'L2_xattn_Wq': 8.0,
     'L2_xattn_Wk': 7.747,
     'L2_xattn_Wv': 7.67,
     'L2_ffn_w_router': 8.0,
     'L2_ffn_wg': 8.0,
     'L2_ffn_wu': 8.0,
     'L2_ffn_wd': 8.0,
     'L2_ffn_sg': 8.0,
     'L2_ffn_su': 8.0,
     'L2_ffn_sd': 8.0,
     'L3_ffn_gate_w': 8.0,
     'L3_ffn_w_gate': 8.0,
     'L3_ffn_w_up': 8.0,
     'L3_ffn_w_down': 8.0,
     'L3_ffn_shgate_w': 8.0,
     'L3_ffn_shw_gate': 8.0,
     'L3_ffn_shw_up': 8.0,
     'L3_ffn_shw_down': 8.0,
     'L3_xattn_Wq': 4.063,
     'L3_xattn_Wk': 3.045}
    for name, (base, spread) in spreads.items():
        noise = np.random.default_rng([zlib.crc32(name.encode()), seed]).standard_normal(out[name].shape)
        drawn = base * np.exp(spread * noise) if base else spread * noise
        out[name] = jnp.asarray(drawn.astype(out[name].dtype))
    for name, factor in factors.items():
        out[name] = (out[name] * factor).astype(out[name].dtype)
    return out
```

```python
from contextlib import ExitStack

import numpy as np

import concourse.bass as bass
from concourse import mybir

F32 = mybir.dt.float32
BF16 = mybir.dt.bfloat16
I32 = mybir.dt.int32
U32 = mybir.dt.uint32
ALU = mybir.AluOpType
ACT = mybir.ActivationFunctionType
AX = mybir.AxisListType

B, S, D = 8, 128, 256
P = 128
DC = D // P
N = B * S
HALF = N // 2
BANKS = 8
LN_EPS = 1e-5

L0_H, L0_HD = 2, 128
GN_EPS = 1e-3
L0_F = 1024
L0_FC = L0_F // P
FP8_MAX = 448.0
L1_H, L1_HD = 16, 8
NEG = 1.0e6
EXPERTS, RANK = 8, 16
LORA_ALPHA = 16.0
L2_H, L2_HD = 32, 8
RMS_EPS = 1e-6
L2_I, L2_SHARED = 640, 2
L3_H, L3_HD = 16, 16
SCORE_LIM = 50.0
RES_SCALE_MAX = 0.3
L3_I, L3_SI = 176, 352


class Steps:

    def __init__(self, engine, semaphore):
        self.engine, self.semaphore, self.count = engine, semaphore, 0

    def mark(self, instruction):
        self.count += 1
        instruction.then_inc(self.semaphore, 1)

    def settle(self):
        self.engine.wait_ge(self.semaphore, self.count)


def over_batches(row, n=B):
    return row.unsqueeze(1).to_broadcast([row.shape[0], n, row.shape[1]])


def over_last(cols, k):
    return cols.unsqueeze(2).to_broadcast([cols.shape[0], cols.shape[1], k])


def row_stats(nc, steps, T, source, eps, var_ready):
    for b in range(B):
        steps.mark(nc.vector.bn_stats(T.bn[:, b, :], source(b)))
    steps.settle()
    for b in range(B):
        steps.mark(nc.vector.bn_aggr(T.mv[:, b, :], T.bn[:, b, :]))
    steps.settle()
    nc.vector.tensor_scalar(T.vareps[:, :], T.mv[:, :, 1], eps, None, ALU.add).then_inc(var_ready, 1)


def normalise(nc, T, source, target, done):
    for b in range(B):
        nc.vector.tensor_scalar(target(b), source(b), T.mv[:, b, 0:1], T.rstd[:, b:b + 1],
                                ALU.subtract, ALU.mult).then_inc(done, 1)


def rstd_on_pool(nc, pool, T, var_ready, rstd_ready, n=1):
    pool.wait_ge(var_ready, n)
    nc.gpsimd.tensor_tensor(T.rstd[:, :], T.vareps[:, :], T.minus_half[:, 0:B], ALU.pow).then_inc(rstd_ready, 1)


def l0_attention(nc, T, sem):
    ctx_in, x_in, ident_in, wh_in, dn_in = map(sem, ("l0a_ctx_in", "l0a_x_in", "l0a_ident_in", "l0a_wh_in", "l0a_dn_in"))
    wg_in, wo_in, gn_in = map(sem, ("l0a_wg_in", "l0a_wo_in", "l0a_gn_in"))
    step, half_set, var_ready, rstd_ready, xn_ready = map(sem, ("l0a_step", "l0a_half_set", "l0a_var", "l0a_rstd", "l0a_xn"))
    ctx_turned, xn_turned, ctxT_ready, xnT_ready = map(sem, ("l0a_ctx_turned", "l0a_xn_turned", "l0a_ctxT", "l0a_xnT"))
    k_mm, q_mm, k_ready, q_ready, v_mm, v_ready = map(sem, ("l0a_k_mm", "l0a_q_mm", "l0a_k", "l0a_q", "l0a_v_mm", "l0a_v"))
    s_mm, a_ready, o_mm, w_mm, w_ready, wy_ready = map(sem, ("l0a_s_mm", "l0a_a", "l0a_o_mm", "l0a_w_mm", "l0a_w", "l0a_wy"))
    wy_turned, wyT_ready, out_mm, gn_done = map(sem, ("l0a_wy_turned", "l0a_wyT", "l0a_out_mm", "l0a_gn_done"))
    X, PS = T.X, T.PS
    KT = T.view(0, L0_H * N).rearrange("p (h n) -> p h n", h=L0_H)
    QT = T.view(2048, L0_H * N).rearrange("p (h n) -> p h n", h=L0_H)
    V = T.view(4096, L0_H * N).rearrange("p (h b e) -> p h b e", h=L0_H, b=B)
    AT = T.view(6144, L0_H * S).rearrange("p (h s) -> p h s", h=L0_H)
    W = T.view(6400, B * D).rearrange("p (b d) -> p b d", b=B)
    Y = T.view(8448, B * D).rearrange("p (b d) -> p b d", b=B)
    WYT = T.view(10496, DC * N).rearrange("p (c n) -> p c n", c=DC)
    O_banks = PS[:, 0:4, :].rearrange("p (h g) (b e) -> p h (g b) e", h=L0_H, b=4)

    with nc.Block() as block:

        @block.sync
        def _(sp):
            for g in range(2):
                sp.dma_start(T.CTX[:, 4 * g:4 * g + 4, :],
                             T.dram["ctx"][4 * g:4 * g + 4].rearrange("b p d -> p b d")).then_inc(ctx_in, 16)
            sp.dma_start(T.Wh[:, :, :], T.dram["Wh"].rearrange("h d e -> d h e")).then_inc(wh_in, 16)
            sp.dma_start(T.wo[:, :, :], T.dram["wo"].rearrange("(c p) n -> p c n", c=DC)).then_inc(wo_in, 16)
            sp.dma_start(T.wfc[:, :, :], T.dram["wfcT"].rearrange("(c p) n -> p c n", c=DC)).then_inc(T.wfc_in, 16)
            sp.dma_start(T.wproj[:, :, :], T.dram["wprojT"].rearrange("(c p) n -> p c n", c=L0_FC)).then_inc(T.wproj_in, 16)

        @block.scalar
        def _(act):
            act.dma_start(T.ident[:, :], T.dram["ident"]).then_inc(ident_in, 16)
            for g in range(2):
                act.dma_start(X[:, 4 * g:4 * g + 4, :],
                              T.dram["x"][4 * g:4 * g + 4].rearrange("b p d -> p b d")).then_inc(x_in, 16)
            act.dma_start(T.DnT[:, :, :], T.dram["dnT"].rearrange("h t s -> t h s")).then_inc(dn_in, 16)
            act.dma_start(T.wg[:, :, :], T.dram["wg"].rearrange("(c p) n -> p c n", c=DC)).then_inc(wg_in, 16)
            act.dma_start(T.gn[:, 0, :], T.dram["gn_gamma"].unsqueeze(0).to_broadcast([P, D])).then_inc(gn_in, 16)
            act.dma_start(T.gn[:, 1, :], T.dram["gn_beta"].unsqueeze(0).to_broadcast([P, D])).then_inc(gn_in, 16)
            for k in range(2 * DC):
                act.wait_ge(ctx_turned, k + 1)
                nc.scalar.activation(T.CTXT[:, k // 2, (k % 2) * HALF:(k % 2 + 1) * HALF], PS[:, k, :],
                                     ACT.Copy).then_inc(ctxT_ready, 1)
            for k in range(2 * L0_H):
                act.wait_ge(k_mm, k + 1)
                nc.scalar.activation(KT[:, k // 2, (k % 2) * HALF:(k % 2 + 1) * HALF], PS[:, k, :],
                                     ACT.Copy).then_inc(k_ready, 1)
            for k in range(2 * DC):
                act.wait_ge(xn_turned, k + 1)
                nc.scalar.activation(T.XNT[:, k // 2, (k % 2) * HALF:(k % 2 + 1) * HALF], PS[:, 4 + k, :],
                                     ACT.Copy).then_inc(xnT_ready, 1)
            for k in range(2 * L0_H):
                act.wait_ge(q_mm, k + 1)
                nc.scalar.activation(QT[:, k // 2, (k % 2) * HALF:(k % 2 + 1) * HALF], PS[:, 4 + k, :],
                                     ACT.Copy).then_inc(q_ready, 1)
            for k in range(4):
                act.wait_ge(w_mm, k + 1)
                nc.scalar.activation(W[:, 2 * k:2 * k + 2, :], PS[:, 4 + k, :].rearrange("p (b d) -> p b d", b=2),
                                     ACT.Relu).then_inc(w_ready, 1)
            for k in range(2 * DC):
                act.wait_ge(wy_turned, k + 1)
                nc.scalar.activation(WYT[:, k // 2, (k % 2) * HALF:(k % 2 + 1) * HALF], PS[:, 4 + k, :],
                                     ACT.Copy).then_inc(wyT_ready, 1)

        @block.gpsimd
        def _(pool):
            nc.gpsimd.memset(T.minus_half[:, :], -0.5).then_inc(half_set, 1)
            pool.wait_ge(half_set, 1)
            pool.wait_ge(ident_in, 16)
            rstd_on_pool(nc, pool, T, var_ready, rstd_ready, 1)
            nc.gpsimd.tensor_copy(T.ident16[:, :], T.ident[:, :]).then_inc(half_set, 1)
            pool.wait_ge(half_set, 2)
            rstd_on_pool(nc, pool, T, var_ready, rstd_ready, 2)

        @block.tensor
        def _(pe):
            pe.wait_ge(ident_in, 16)
            pe.wait_ge(ctx_in, 32)
            for c in range(DC):
                for b in range(B):
                    t = nc.tensor.transpose(PS[:, 2 * c + b // 4, (b % 4) * P:(b % 4 + 1) * P],
                                            T.CTX[:, b, c * P:(c + 1) * P], T.ident[:, :])
                    if b % 4 == 3:
                        t.then_inc(ctx_turned, 1)
            pe.wait_ge(wh_in, 16)
            for h in range(L0_H):
                for g in range(2):
                    pe.wait_ge(ctxT_ready, 2 * h + g + 1)
                    nc.tensor.matmul(PS[:, 2 * h + g, :], T.Wh[:, h, :], T.CTXT[:, h, g * HALF:(g + 1) * HALF],
                                     start=True, stop=True).then_inc(k_mm, 1)
            for c in range(DC):
                for b in range(B):
                    if c == 0:
                        pe.wait_ge(xn_ready, b + 1)
                    t = nc.tensor.transpose(PS[:, 4 + 2 * c + b // 4, (b % 4) * P:(b % 4 + 1) * P],
                                            T.XN[:, b, c * P:(c + 1) * P], T.ident[:, :])
                    if b % 4 == 3:
                        t.then_inc(xn_turned, 1)
            pe.wait_ge(k_ready, 4)
            for h in range(L0_H):
                for b in range(B):
                    t = nc.tensor.matmul(PS[:, 2 * h + b // 4, (b % 4) * P:(b % 4 + 1) * P],
                                         T.CTXT[:, h, b * S:(b + 1) * S], T.Wh[:, h, :], start=True, stop=True)
                    if b % 4 == 3:
                        t.then_inc(v_mm, 1)
            for h in range(L0_H):
                for g in range(2):
                    pe.wait_ge(xnT_ready, 2 * h + g + 1)
                    nc.tensor.matmul(PS[:, 4 + 2 * h + g, :], T.Wh[:, h, :], T.XNT[:, h, g * HALF:(g + 1) * HALF],
                                     start=True, stop=True).then_inc(q_mm, 1)
            pe.wait_ge(v_ready, 4)
            for h in range(L0_H):
                pe.wait_ge(q_ready, 2 * h + 2)
                for b in range(B):
                    t = nc.tensor.matmul(PS[:, h, 0:S], KT[:, h, b * S:(b + 1) * S], QT[:, h, b * S:(b + 1) * S],
                                         start=(b == 0), stop=(b == B - 1))
                t.then_inc(s_mm, 1)
            pe.wait_ge(q_ready, 4)
            pe.wait_ge(wg_in, 16)
            for b in range(B):
                for c in range(DC):
                    t = nc.tensor.matmul(PS[:, 4 + b // 2, (b % 2) * D:(b % 2 + 1) * D], T.XNT[:, c, b * S:(b + 1) * S],
                                         T.wg[:, c, :], start=(c == 0), stop=(c == DC - 1))
                if b % 2:
                    t.then_inc(w_mm, 1)
            for h in range(L0_H):
                pe.wait_ge(a_ready, 2)
                for g in range(2):
                    nc.tensor.matmul(PS[:, 2 * h + g, :], AT[:, h, :],
                                     V[:, h, 4 * g:4 * g + 4, :].rearrange("p b e -> p (b e)"),
                                     start=True, stop=True).then_inc(o_mm, 1)
            pe.wait_ge(w_ready, 4)
            for c in range(DC):
                for b in range(B):
                    if c == 0:
                        pe.wait_ge(wy_ready, b + 1)
                    t = nc.tensor.transpose(PS[:, 4 + 2 * c + b // 4, (b % 4) * P:(b % 4 + 1) * P],
                                            Y[:, b, c * P:(c + 1) * P], T.ident[:, :])
                    if b % 4 == 3:
                        t.then_inc(wy_turned, 1)
            pe.wait_ge(wo_in, 16)
            pe.wait_ge(wyT_ready, 4)
            for b in range(B):
                for c in range(DC):
                    t = nc.tensor.matmul(PS[:, b // 2, (b % 2) * D:(b % 2 + 1) * D], WYT[:, c, b * S:(b + 1) * S],
                                         T.wo[:, c, :], start=(c == 0), stop=(c == DC - 1))
                if b % 2:
                    t.then_inc(out_mm, 1)

        @block.vector
        def _(dve):
            steps = Steps(dve, step)
            dve.wait_ge(x_in, 32)
            row_stats(nc, steps, T, lambda b: X[:, b, :], LN_EPS, var_ready)
            dve.wait_ge(rstd_ready, 1)
            normalise(nc, T, lambda b: X[:, b, :], lambda b: T.XN[:, b, :], xn_ready)
            for k in range(4):
                dve.wait_ge(v_mm, k + 1)
                nc.vector.tensor_copy(V[:, k // 2, 4 * (k % 2):4 * (k % 2) + 4, :],
                                      PS[:, k, :].rearrange("p (b e) -> p b e", b=4)).then_inc(v_ready, 1)
            dve.wait_ge(s_mm, 2)
            dve.wait_ge(dn_in, 16)
            steps.mark(nc.vector.tensor_tensor(AT[:, :, :], PS[:, 0:2, 0:S], T.DnT[:, :, :], ALU.mult))
            steps.settle()
            steps.mark(nc.vector.scalar_tensor_tensor(out=AT[:, :, :], in0=AT[:, :, :], scalar=-1.0, in1=AT[:, :, :],
                                                      op0=ALU.mult, op1=ALU.max))
            steps.settle()
            nc.vector.tensor_scalar(AT[:, :, :], AT[:, :, :], 1.0, None, ALU.max).then_inc(a_ready, 2)
            dve.wait_ge(o_mm, 4)
            row_stats(nc, steps, T, lambda b: O_banks[:, :, b, :], GN_EPS, var_ready)
            dve.wait_ge(rstd_ready, 2)
            for b in range(B):
                steps.mark(nc.vector.tensor_scalar(Y[:, b, :].rearrange("p (h e) -> p h e", h=L0_H), O_banks[:, :, b, :],
                                                   T.mv[:, b, 0:1], T.rstd[:, b:b + 1], ALU.subtract, ALU.mult))
            steps.settle()
            dve.wait_ge(gn_in, 32)
            steps.mark(nc.vector.tensor_tensor(Y[:, :, :], Y[:, :, :], over_batches(T.gn[:, 0, :]), ALU.mult))
            steps.settle()
            steps.mark(nc.vector.tensor_tensor(Y[:, :, :], Y[:, :, :], over_batches(T.gn[:, 1, :]), ALU.add))
            steps.settle()
            dve.wait_ge(w_ready, 4)
            for b in range(B):
                nc.vector.tensor_tensor(Y[:, b, :], Y[:, b, :], W[:, b, :], ALU.mult).then_inc(wy_ready, 1)
            for k in range(4):
                dve.wait_ge(out_mm, k + 1)
                nc.vector.tensor_tensor(X[:, 2 * k:2 * k + 2, :], X[:, 2 * k:2 * k + 2, :],
                                        PS[:, k, :].rearrange("p (b d) -> p b d", b=2), ALU.add).then_inc(gn_done, 1)
            dve.wait_ge(gn_done, 4)


EXP_BITS = 0x7F800000
FP8_MIN_NORMAL = 2.0 ** -6
FP8_GRID = 1.5 * 2.0 ** 20


def to_fp8_grid(nc, steps, v, magic, out):
    steps.mark(nc.vector.tensor_scalar(magic.bitcast(U32), v.bitcast(U32), EXP_BITS, None, ALU.bitwise_and))
    steps.settle()
    steps.mark(nc.vector.tensor_scalar(magic, magic, FP8_MIN_NORMAL, FP8_GRID, ALU.max, ALU.mult))
    steps.settle()
    steps.mark(nc.vector.tensor_tensor(v, v, magic, ALU.add))
    steps.settle()
    return nc.vector.tensor_tensor(out, v, magic, ALU.subtract)


def l0_ffn(nc, T, sem):
    step, var_ready, rstd_ready, xn_ready = map(sem, ("l0f_step", "l0f_var", "l0f_rstd", "l0f_xn"))
    amax_ready, amax_turned, scale_ready, scale_spread = map(sem, ("l0f_amax", "l0f_amax_turned", "l0f_scale", "l0f_spread"))
    dequant_ready, x8_ready, x8_turned, x8T_ready = map(sem, ("l0f_dequant", "l0f_x8", "l0f_x8_turned", "l0f_x8T"))
    wfc8_ready, wproj8_ready, fc_mm, r_ready, h_ready = map(sem, ("l0f_wfc8", "l0f_wproj8", "l0f_fc_mm", "l0f_r", "l0f_h"))
    inv_ready, v_ready, h8_ready, proj_mm, x_done = map(sem, ("l0f_inv", "l0f_v", "l0f_h8", "l0f_proj_mm", "l0f_x"))
    X, PS = T.X, T.PS
    H = T.view(0, L0_FC * N).rearrange("p (f n) -> p f n", f=L0_FC)
    H8 = T.view(8192, L0_FC * N // 2).bitcast(BF16).rearrange("p (f n) -> p f n", f=L0_FC)
    V = T.view(12288, 2048)
    MAGIC = T.view(14336, 2048)
    X8 = T.view(16384, 1024).bitcast(BF16).rearrange("p (b d) -> p b d", b=B)
    X8T = T.view(17408, 1024).bitcast(BF16).rearrange("p (c n) -> p c n", c=DC)
    WFC8 = T.view(18432, 1024).bitcast(BF16).rearrange("p (c n) -> p c n", c=DC)
    WPROJ8 = T.view(19456, 1024).bitcast(BF16).rearrange("p (f d) -> p f d", f=L0_FC)
    SC = T.view(20480, 64)
    amax = SC[:, 0:4]
    top = SC[0:1, 4:8]
    scale = SC[:, 8:12]
    inv = SC[:, 12:16]
    deq = SC[:, 16:18]
    magics = T.view(20544, 2 * N).rearrange("p (k n) -> p k n", k=2)

    with nc.Block() as block:

        @block.gpsimd
        def _(pool):
            rstd_on_pool(nc, pool, T, var_ready, rstd_ready, 1)

        @block.tensor
        def _(pe):
            def spread_max(k, first, count):
                pe.wait_ge(amax_ready, k)
                for m in range(count):
                    t = nc.tensor.transpose(PS[0:1, 7, m * P:(m + 1) * P], amax[:, first + m:first + m + 1], T.ident[:, :])
                t.then_inc(amax_turned, 1)
                pe.wait_ge(scale_ready, k)
                nc.tensor.matmul(PS[:, 6, first:first + count], T.ones[0:1, :], top[:, first:first + count],
                                 start=True, stop=True).then_inc(scale_spread, 1)

            spread_max(1, 0, 2)
            spread_max(2, 2, 1)
            ps8 = PS[:, 0:2, :].bitcast(BF16).rearrange("p c (b t) -> p c b t", b=B)
            for b in range(B):
                pe.wait_ge(x8_ready, 1)
                for c in range(DC):
                    t = nc.tensor.transpose(ps8[:, c, b, :], X8[:, b, c * P:(c + 1) * P], T.ident16[:, :])
            t.then_inc(x8_turned, 1)
            pe.wait_ge(x8T_ready, 2)
            pe.wait_ge(wfc8_ready, 1)
            for k in range(2 * L0_FC):
                if k >= 6:
                    pe.wait_ge(r_ready, k - 5)
                for c in range(DC):
                    t = nc.tensor.matmul(PS[:, k % 6, :], WFC8[:, c, (k // 2) * P:(k // 2 + 1) * P],
                                         X8T[:, c, (k % 2) * HALF:(k % 2 + 1) * HALF], start=(c == 0), stop=(c == DC - 1))
                t.then_inc(fc_mm, 1)
            spread_max(3, 3, 1)
            pe.wait_ge(wproj8_ready, 1)
            pe.wait_ge(r_ready, 2 * L0_FC)
            pe.wait_ge(h8_ready, L0_FC)
            for b in range(B):
                for f in range(L0_FC):
                    t = nc.tensor.matmul(PS[:, b // 2, (b % 2) * D:(b % 2 + 1) * D], H8[:, f, b * S:(b + 1) * S],
                                         WPROJ8[:, f, :], start=(f == 0), stop=(f == L0_FC - 1))
                if b % 2:
                    t.then_inc(proj_mm, 1)

        @block.scalar
        def _(act):
            act.wait_ge(x8_turned, 1)
            for c in range(DC):
                nc.scalar.activation(X8T[:, c, :], PS[:, c, :].bitcast(BF16), ACT.Copy).then_inc(x8T_ready, 1)
            act.wait_ge(dequant_ready, 1)
            for k in range(2 * L0_FC):
                act.wait_ge(fc_mm, k + 1)
                nc.scalar.activation(H[:, k // 2, (k % 2) * HALF:(k % 2 + 1) * HALF], PS[:, k % 6, :], ACT.Relu,
                                     scale=deq[:, 0:1]).then_inc(r_ready, 1)
            act.wait_ge(inv_ready, 3)
            for f in range(L0_FC):
                act.wait_ge(h_ready, f + 1)
                nc.scalar.activation(H[:, f, :], H[:, f, :], ACT.Copy, scale=inv[:, 3:4]).then_inc(v_ready, 1)

        @block.vector
        def _(dve):
            steps = Steps(dve, step)

            def scales(k, first, count):
                dve.wait_ge(amax_turned, k)
                steps.mark(nc.vector.tensor_reduce(top[:, first:first + count],
                                                   PS[0:1, 7, 0:count * P].rearrange("p (m q) -> p m q", m=count), AX.X, ALU.max))
                steps.settle()
                if first == 3:
                    steps.mark(nc.vector.tensor_tensor(top[:, 3:4], top[:, 3:4], top[:, 3:4], ALU.mult))
                    steps.settle()
                nc.vector.tensor_scalar(top[:, first:first + count], top[:, first:first + count],
                                        1.0 / FP8_MAX, 1e-6, ALU.mult, ALU.max).then_inc(scale_ready, 1)
                dve.wait_ge(scale_spread, k)
                steps.mark(nc.vector.tensor_copy(scale[:, first:first + count], PS[:, 6, first:first + count]))
                steps.settle()
                nc.vector.reciprocal(inv[:, first:first + count], scale[:, first:first + count]).then_inc(inv_ready, 1)
                dve.wait_ge(inv_ready, k)

            row_stats(nc, steps, T, lambda b: X[:, b, :], LN_EPS, var_ready)
            dve.wait_ge(T.wfc_in, 16)
            steps.mark(nc.vector.tensor_reduce(amax[:, 0:1], T.wfc[:, :, :], AX.XY, ALU.max, apply_absolute_value=True))
            dve.wait_ge(T.wproj_in, 16)
            nc.vector.tensor_reduce(amax[:, 1:2], T.wproj[:, :, :], AX.XY, ALU.max,
                                    apply_absolute_value=True).then_inc(amax_ready, 1)
            dve.wait_ge(rstd_ready, 1)
            normalise(nc, T, lambda b: X[:, b, :], lambda b: T.XN[:, b, :], xn_ready)
            scales(1, 0, 2)
            dve.wait_ge(xn_ready, B)
            nc.vector.tensor_reduce(amax[:, 2:3], T.XN[:, :, :], AX.XY, ALU.max,
                                    apply_absolute_value=True).then_inc(amax_ready, 1)
            steps.mark(nc.vector.tensor_scalar(V[:, :], T.wfc[:, :, :].rearrange("p c n -> p (c n)"), inv[:, 0:1], None, ALU.mult))
            steps.settle()
            to_fp8_grid(nc, steps, V[:, :], MAGIC[:, :], WFC8[:, :, :].rearrange("p c n -> p (c n)")).then_inc(wfc8_ready, 1)
            dve.wait_ge(wfc8_ready, 1)
            scales(2, 2, 1)
            steps.mark(nc.vector.tensor_scalar(V[:, :], T.XN[:, :, :].rearrange("p b d -> p (b d)"), inv[:, 2:3], None, ALU.mult))
            steps.settle()
            to_fp8_grid(nc, steps, V[:, :], MAGIC[:, :], X8[:, :, :].rearrange("p b d -> p (b d)")).then_inc(x8_ready, 1)
            nc.vector.tensor_tensor(deq[:, 0:1], scale[:, 0:1], scale[:, 2:3], ALU.mult).then_inc(dequant_ready, 1)
            dve.wait_ge(x8_ready, 1)
            steps.mark(nc.vector.tensor_scalar(V[:, :], T.wproj[:, :, :].rearrange("p f d -> p (f d)"), inv[:, 1:2], None, ALU.mult))
            steps.settle()
            to_fp8_grid(nc, steps, V[:, :], MAGIC[:, :], WPROJ8[:, :, :].rearrange("p f d -> p (f d)")).then_inc(wproj8_ready, 1)
            for f in range(L0_FC):
                dve.wait_ge(r_ready, 2 * f + 2)
                steps.mark(nc.vector.tensor_reduce(SC[:, 24 + f:25 + f], H[:, f, :], AX.X, ALU.max))
                steps.settle()
                nc.vector.tensor_tensor(H[:, f, :], H[:, f, :], H[:, f, :], ALU.mult).then_inc(h_ready, 1)
            nc.vector.tensor_reduce(amax[:, 3:4], SC[:, 24:24 + L0_FC], AX.X, ALU.max).then_inc(amax_ready, 1)
            scales(3, 3, 1)
            steps.mark(nc.vector.tensor_tensor(deq[:, 1:2], scale[:, 1:2], scale[:, 3:4], ALU.mult))
            for f in range(L0_FC):
                dve.wait_ge(v_ready, f + 1)
                if f:
                    dve.wait_ge(h8_ready, f)
                to_fp8_grid(nc, steps, H[:, f, :], magics[:, f % 2, :], H8[:, f, :]).then_inc(h8_ready, 1)
            for k in range(4):
                dve.wait_ge(proj_mm, k + 1)
                xk = X[:, 2 * k:2 * k + 2, :].rearrange("p b d -> p (b d)")
                nc.vector.scalar_tensor_tensor(out=xk, in0=PS[:, k, :], scalar=deq[:, 1:2], in1=xk,
                                               op0=ALU.mult, op1=ALU.add).then_inc(x_done, 1)
            dve.wait_ge(x_done, 4)


PARTS = 3
STACK = PARTS * PARTS * L1_HD
BIAS_ROW = STACK
MAX_ROW = STACK + 1
STACK_ALL = MAX_ROW + PARTS
ONES_FROM = 64
POS = D
PC = POS // P
GROUPS = 4
V_PITCH = P + L1_HD


def split_rest(nc, steps, whole, first, second, third, done):
    steps.mark(nc.vector.tensor_tensor(whole, whole, first, ALU.subtract))
    steps.settle()
    steps.mark(nc.vector.tensor_copy(second, whole))
    steps.settle()
    nc.vector.tensor_tensor(third, whole, second, ALU.subtract).then_inc(done, 1)


def l1_attention(nc, T, sem):
    step, var_ready, rstd_ready, xn_ready = map(sem, ("l1a_step", "l1a_var", "l1a_rstd", "l1a_xn"))
    w_in, mask_in, mask_turned, mask_ready, const_ready = map(sem, ("l1a_w_in", "l1a_mask_in", "l1a_mask_turned", "l1a_mask", "l1a_const"))
    k_mm, q_mm, v_mm, k_copied, q_copied, v_ready = map(sem, ("l1a_k_mm", "l1a_q_mm", "l1a_v_mm", "l1a_k_copied", "l1a_q_copied", "l1a_v"))
    k_split, q_split = map(sem, ("l1a_k_split", "l1a_q_split"))
    stack_in = [sem(f"l1a_stack_in{n}") for n in range(4)]
    k_written, q_written = sem("l1a_k_written"), [sem(f"l1a_q_written{n}") for n in range(4)]
    maxrow_in = [sem("l1a_maxrow_in0"), sem("l1a_maxrow_in1")]
    probe_mm, probe_read, maxT_ready = map(sem, ("l1a_probe_mm", "l1a_probe_read", "l1a_maxT"))
    score_mm, exp_ready, pv_mm, att_ready, x_done = map(sem, ("l1a_score_mm", "l1a_exp", "l1a_pv_mm", "l1a_att", "l1a_x"))
    den_read = sem("l1a_den_read")
    X, PS = T.X, T.PS

    BUFS = 4
    at = [0]

    def take(cols, dt=F32):
        v = T.view(at[0], cols)
        at[0] += cols
        return v if dt == F32 else v.bitcast(dt)

    W3 = take(3 * P).rearrange("p (w o) -> p w o", w=3)
    BQK = take(2)
    BV = take(P)
    MASKROW = take(P)
    MASKCOL = take(B * PC)
    MASKB = take(B * POS).rearrange("p (b t) -> p b t", b=B)
    NEGROW = take(B * POS // 2, BF16)
    K = T.XNT[:, :, :].rearrange("p c n -> p (c n)")
    Q = T.XN[:, :, :].rearrange("p b t -> p (b t)")
    KP = [take(B * POS // 2, BF16) for _ in range(PARTS)]
    QP = [take(B * POS // 2, BF16) for _ in range(PARTS)]
    KS = [take(L1_H * POS // 2, BF16).rearrange("p (h t) -> p h t", h=L1_H) for _ in range(BUFS)]
    QS = [take(L1_H * POS // 2, BF16).rearrange("p (h t) -> p h t", h=L1_H) for _ in range(BUFS)]
    padded = take((B * PC + 1) * GROUPS * V_PITCH)
    VZ = [padded[:, n * GROUPS * V_PITCH:(n + 1) * GROUPS * V_PITCH] for n in range(B * PC)]
    OZ = padded[:, B * PC * GROUPS * V_PITCH:]
    VT = take(2 * P).rearrange("p (r o) -> p r o", r=2)
    ring = take(4 * GROUPS * POS)
    E = ring.rearrange("p (s j t) -> p s j t", s=4, j=GROUPS)
    NEGF = ring[:, 0:B * POS]
    MX = take(B * L1_H * PC).rearrange("p (b k) -> p b k", b=B)
    MT = take(2 * P).rearrange("p (r t) -> p r t", r=2)
    MTP = take(2 * PARTS * P // 2, BF16).rearrange("p (r i t) -> p r i t", r=2, i=PARTS)
    REC = take(2 * POS).rearrange("p (r t) -> p r t", r=2)
    ATT = take(2 * POS).rearrange("p (r t) -> p r t", r=2)
    assert at[0] <= ARENA, at[0]
    STEPS_B = GROUPS * PC
    MK = L1_H * PC
    RING = L1_H + 1
    LAG = 2
    SCALE = float(L1_HD) ** -0.5

    with nc.Block() as block:

        @block.sync
        def _(sp):
            sp.dma_start(W3[:, :, :], T.dram["l1_w"]).then_inc(w_in, 16)
            sp.dma_start(BQK[:, :], T.dram["l1_bqk"]).then_inc(w_in, 16)
            sp.dma_start(BV[:, :], T.dram["l1_bv"].unsqueeze(0).to_broadcast([P, P])).then_inc(w_in, 16)
            sp.dma_start(MASKROW[0:B * PC, :], T.dram["mask"].rearrange("b o (c p) -> (b o c) p", c=PC)).then_inc(mask_in, 16)
            sp.dma_start(NEGF[0:1, :], T.dram["mask"].rearrange("b o t -> o (b t)")).then_inc(mask_in, 16)
            sp.dma_start(MASKB[:, :, :], T.dram["mask"].rearrange("b o t -> o b t").to_broadcast([P, B, POS])).then_inc(mask_in, 16)
            sp.wait_ge(const_ready, 8)
            sp.wait_ge(mask_ready, 2)

            def write_parts(parts, scratch, b, written):
                for i in range(PARTS):
                    sp.dma_start(scratch[b, i].rearrange("d h t -> h d t"),
                                 parts[i][:, b * POS:(b + 1) * POS]).then_inc(written, 16)

            def load_stacks(b):
                if b >= BUFS:
                    sp.wait_ge(score_mm, STEPS_B * (b - BUFS + 1))
                sp.wait_ge(q_written[b % BUFS], 16 * PARTS * (b // BUFS + 1))
                for m in range(PARTS):
                    rows = slice(PARTS * L1_HD * m, PARTS * L1_HD * (m + 1))
                    sp.dma_start(KS[b % BUFS][rows].rearrange("p h t -> p (h t)"),
                                 T.scr_k[b].rearrange("i d h t -> (i d) (h t)")).then_inc(stack_in[b % BUFS], 16)
                    sp.dma_start(QS[b % BUFS][rows].rearrange("p h t -> p (h t)"),
                                 T.scr_q[b, m].rearrange("d h t -> d (h t)").unsqueeze(0)
                                 .to_broadcast([PARTS, L1_HD, L1_H * POS])).then_inc(stack_in[b % BUFS], 16)
                sp.dma_start(KS[b % BUFS][BIAS_ROW:BIAS_ROW + 1],
                             NEGROW[0:1, b * POS:(b + 1) * POS].unsqueeze(1)
                             .to_broadcast([1, L1_H, POS])).then_inc(stack_in[b % BUFS], 16)

            def load_max(b):
                sp.wait_ge(maxT_ready, b + 1)
                for i in range(PARTS):
                    sp.dma_start(QS[b % BUFS][MAX_ROW + i:MAX_ROW + i + 1].rearrange("a h (c t) -> a (h c) t", c=PC),
                                 MTP[0:MK, b % 2, i, :]).then_inc(maxrow_in[b % 2], 16)

            for b in range(B):
                sp.wait_ge(k_split, b // 2 + 1)
                write_parts(KP, T.scr_k, b, k_written)
            sp.wait_ge(k_written, 16 * PARTS * B)
            for b in range(BUFS):
                sp.wait_ge(q_split, b // 2 + 1)
                write_parts(QP, T.scr_q, b, q_written[b])
                if b:
                    load_stacks(b - 1)
            load_stacks(BUFS - 1)
            for b in range(BUFS, B):
                sp.wait_ge(q_split, b // 2 + 1)
                write_parts(QP, T.scr_q, b, q_written[b % BUFS])
            for b in range(B):
                load_max(b)
                if 1 <= b <= B - BUFS:
                    load_stacks(b + BUFS - 1)

        @block.gpsimd
        def _(pool):
            for s in (*KS, *QS):
                nc.gpsimd.memset(s[ONES_FROM:96], 1.0).then_inc(const_ready, 1)
            pool.wait_ge(const_ready, 2 * BUFS)
            rstd_on_pool(nc, pool, T, var_ready, rstd_ready)
            for b in range(B):
                pool.wait_ge(att_ready, b + 1)
                nc.gpsimd.tensor_tensor(X[:, b, :], X[:, b, :], ATT[:, b % 2, :], ALU.add).then_inc(x_done, 1)
            pool.wait_ge(x_done, B)

        @block.tensor
        def _(pe):
            pe.wait_ge(mask_in, 48)
            nc.tensor.transpose(PS[:, 0, 0:B * PC], MASKROW[0:B * PC, :], T.ident[0:B * PC, 0:B * PC]).then_inc(mask_turned, 1)
            pe.wait_ge(w_in, 48)
            for p in range(4):
                nc.tensor.matmul(PS[:, 4 + p, :], W3[:, 1, :], T.CTX[:, 2 * p:2 * p + 2, :].rearrange("p b t -> p (b t)"),
                                 start=True, stop=True).then_inc(k_mm, 1)
            pe.wait_ge(mask_ready, 1)
            for n in range(B * PC):
                nc.tensor.matmul(PS[:, n // 4, (n % 4) * P:(n % 4 + 1) * P],
                                 T.CTX[:, n // PC, (n % PC) * P:(n % PC + 1) * P], W3[:, 2, :],
                                 start=True, stop=True).then_inc(v_mm, 1)
            for p in range(4):
                pe.wait_ge(k_copied, 2 * p + 2)
                pe.wait_ge(xn_ready, 2 * p + 2)
                nc.tensor.matmul(PS[:, 4 + p, :], W3[:, 0, :], T.XN[:, 2 * p:2 * p + 2, :].rearrange("p b t -> p (b t)"),
                                 start=True, stop=True).then_inc(q_mm, 1)
            pe.wait_ge(v_ready, B * PC)
            pe.wait_ge(q_copied, 8)

            def probe(b, k):
                n = RING * b + k
                if n >= 2:
                    pe.wait_ge(probe_read, n - 1)
                if k == 0:
                    pe.wait_ge(stack_in[b % BUFS], 16 * (2 * PARTS + 1) * (b // BUFS + 1))
                for tc in range(PC):
                    t = nc.tensor.matmul(PS[:, n % 2, tc * POS:(tc + 1) * POS],
                                         QS[b % BUFS][0:MAX_ROW, k, tc * P:(tc + 1) * P],
                                         KS[b % BUFS][0:MAX_ROW, k, :], start=True, stop=True)
                t.then_inc(probe_mm, 1)

            def turn_max(b):
                n = RING * b + L1_H
                pe.wait_ge(probe_read, n)
                nc.tensor.transpose(PS[0:MK, n % 2, 0:P], MX[:, b, :], T.ident[:, :]).then_inc(probe_mm, 1)

            def scores(b, i):
                n = STEPS_B * b + i
                g, c = i // PC, i % PC
                if n >= 2:
                    pe.wait_ge(exp_ready, n - 1)
                if i == 0:
                    pe.wait_ge(maxrow_in[b % 2], 48 * (b // 2 + 1))
                for j in range(4):
                    h = 4 * j + g
                    t = nc.tensor.matmul(PS[:, 2 + 2 * (n % 2) + j // 2, (j % 2) * POS:(j % 2 + 1) * POS],
                                         KS[b % BUFS][0:STACK_ALL, h, c * P:(c + 1) * P],
                                         QS[b % BUFS][0:STACK_ALL, h, :], start=True, stop=True)
                t.then_inc(score_mm, 1)

            def weigh(b, i):
                n = STEPS_B * b + i
                g, c = i // PC, i % PC
                pe.wait_ge(exp_ready, n + 1)
                if i == 0 and b:
                    pe.wait_ge(den_read, b)
                for bank, tile in ((6, VZ[b * PC + c]), (7, OZ)):
                    for j in range(4):
                        t = nc.tensor.matmul(PS[32 * j:32 * j + 32, bank, (b % 2) * POS:(b % 2 + 1) * POS],
                                             tile[:, g * P + 32 * j:g * P + 32 * j + 32], E[:, n % 4, j, :],
                                             start=(i == 0), stop=(i == STEPS_B - 1))
                t.then_inc(pv_mm, 1)

            for k in range(L1_H):
                probe(0, k)
            turn_max(0)
            for b in range(B):
                todo = list(range(L1_H)) if b + 1 < B else []
                for i in range(STEPS_B):
                    scores(b, i)
                    for k in todo[:3]:
                        probe(b + 1, k)
                    todo = todo[3:]
                    if i == 6 and b + 1 < B:
                        turn_max(b + 1)
                    n = STEPS_B * b + i - LAG
                    if n >= 0:
                        weigh(n // STEPS_B, n % STEPS_B)
            for n in range(B * STEPS_B - LAG, B * STEPS_B):
                weigh(n // STEPS_B, n % STEPS_B)

        @block.scalar
        def _(act):
            for mm, copied, whole, first, col in ((k_mm, k_copied, K, KP[0], 1), (q_mm, q_copied, Q, QP[0], 0)):
                for p in range(4):
                    act.wait_ge(mm, p + 1)
                    for target in (whole, first):
                        nc.scalar.activation(target[:, p * 512:(p + 1) * 512], PS[:, 4 + p, :], ACT.Identity,
                                             bias=BQK[:, col:col + 1]).then_inc(copied, 1)
            for n in range(B * STEPS_B):
                act.wait_ge(score_mm, n + 1)
                if n >= 4:
                    act.wait_ge(pv_mm, n - 3)
                nc.scalar.activation(E[:, n % 4, :, :].rearrange("p (a b) t -> p a (b t)", a=2),
                                     PS[:, 2 + 2 * (n % 2):4 + 2 * (n % 2), :], ACT.Exp, scale=SCALE).then_inc(exp_ready, 1)

        @block.vector
        def _(dve):
            steps = Steps(dve, step)
            row_stats(nc, steps, T, lambda b: X[:, b, :], LN_EPS, var_ready)
            steps.mark(nc.vector.memset(padded[:, :], 0.0))
            dve.wait_ge(mask_turned, 1)
            nc.vector.tensor_copy(MASKCOL[:, :], PS[:, 0, 0:B * PC]).then_inc(mask_ready, 1)
            nc.vector.tensor_scalar(NEGROW[0:1, :], NEGF[0:1, :], 1.0, NEG / SCALE, ALU.subtract, ALU.mult).then_inc(mask_ready, 1)
            dve.wait_ge(mask_ready, 2)
            steps.settle()
            ones_at = OZ[:, :].rearrange("p (g x) -> p g x", x=V_PITCH)[:, :, 0:P].rearrange("p g (j r) -> p g j r", r=32)
            for g in range(GROUPS):
                steps.mark(nc.vector.memset(ones_at[:, g, :, 0:L1_HD], 1.0))
            dve.wait_ge(rstd_ready, 1)
            normalise(nc, T, lambda b: X[:, b, :], lambda b: T.XN[:, b, :], xn_ready)
            for p in range(4):
                dve.wait_ge(k_copied, 2 * p + 2)
                cols = slice(p * 512, (p + 1) * 512)
                split_rest(nc, steps, K[:, cols], KP[0][:, cols], KP[1][:, cols], KP[2][:, cols], k_split)
            for p in range(4):
                dve.wait_ge(q_copied, 2 * p + 2)
                cols = slice(p * 512, (p + 1) * 512)
                split_rest(nc, steps, Q[:, cols], QP[0][:, cols], QP[1][:, cols], QP[2][:, cols], q_split)
            for n in range(B * PC):
                dve.wait_ge(v_mm, n + 1)
                v = PS[:, n // 4, (n % 4) * P:(n % 4 + 1) * P]
                steps.mark(nc.vector.tensor_tensor(VT[:, n % 2, :], v, BV[:, :], ALU.add))
                steps.settle()
                target = VZ[n][:, :].rearrange("p (g x) -> p g x", x=V_PITCH)[:, :, 0:P].rearrange("p g (j r) -> p g j r", r=32)[:, :, :, 0:L1_HD]
                nc.vector.tensor_scalar(target, VT[:, n % 2, :].rearrange("p (j g d) -> p g j d", j=4, g=GROUPS), MASKCOL[:, n:n + 1], None,
                                        ALU.mult).then_inc(v_ready, 1)

            def head_max(b, k):
                n = RING * b + k
                dve.wait_ge(probe_mm, n + 1)
                nc.vector.tensor_reduce(MX[:, b, PC * k:PC * k + PC], PS[:, n % 2, :].rearrange("p (c s) -> p c s", c=PC),
                                        AX.X, ALU.max).then_inc(probe_read, 1)

            def max_parts(b):
                n = RING * b + L1_H
                r = b % 2
                dve.wait_ge(probe_mm, n + 1)
                if b >= 2:
                    dve.wait_ge(maxrow_in[r], 48 * (b // 2))
                nc.vector.tensor_scalar(MT[0:MK, r, :], PS[0:MK, n % 2, 0:P], -1.0, None, ALU.mult).then_inc(probe_read, 1)
                dve.wait_ge(probe_read, n + 1)
                steps.mark(nc.vector.tensor_copy(MTP[0:MK, r, 0, :], MT[0:MK, r, :]))
                steps.settle()
                split_rest(nc, steps, MT[0:MK, r, :], MTP[0:MK, r, 0, :], MTP[0:MK, r, 1, :], MTP[0:MK, r, 2, :], maxT_ready)

            def attended(b):
                r = b % 2
                dve.wait_ge(pv_mm, STEPS_B * (b + 1))
                if b >= 2:
                    dve.wait_ge(x_done, b - 1)
                steps.mark(nc.vector.reciprocal(REC[:, r, :], PS[:, 7, r * POS:(r + 1) * POS]))
                steps.settle()
                nc.vector.tensor_tensor(ATT[:, r, :], PS[:, 6, r * POS:(r + 1) * POS], REC[:, r, :], ALU.mult).then_inc(den_read, 1)
                dve.wait_ge(den_read, b + 1)
                nc.vector.tensor_tensor(ATT[:, r, :], ATT[:, r, :], MASKB[:, b, :], ALU.mult).then_inc(att_ready, 1)

            for k in range(L1_H):
                head_max(0, k)
            max_parts(0)
            for b in range(B):
                if b + 1 < B:
                    for k in range(L1_H):
                        head_max(b + 1, k)
                        if k == 3 * LAG - 1 and b:
                            attended(b - 1)
                    max_parts(b + 1)
            attended(B - 2)
            attended(B - 1)


def first_max(nc, steps, scores, top, onehot, tie, priority):
    steps.mark(nc.vector.tensor_reduce(top, scores, AX.X, ALU.max))
    steps.settle()
    steps.mark(nc.vector.tensor_tensor(onehot, scores, over_last(top, EXPERTS), ALU.is_equal))
    steps.settle()
    steps.mark(nc.vector.tensor_tensor(onehot, onehot, over_batches(priority), ALU.mult))
    steps.settle()
    steps.mark(nc.vector.tensor_reduce(tie, onehot, AX.X, ALU.max))
    steps.settle()
    steps.mark(nc.vector.tensor_tensor(onehot, onehot, over_last(tie, EXPERTS), ALU.is_equal))
    steps.settle()


def top_two(nc, steps, R):
    first_max(nc, steps, R.scores, R.top[:, 0, :], R.onehot[:, 0], R.tie, R.priority)
    steps.mark(nc.vector.scalar_tensor_tensor(out=R.scores, in0=R.onehot[:, 0], scalar=-1e30, in1=R.scores,
                                              op0=ALU.mult, op1=ALU.add))
    steps.settle()
    first_max(nc, steps, R.scores, R.top[:, 1, :], R.onehot[:, 1], R.tie, R.priority)


def combine(nc, steps, R, out, scale, done):
    for k in range(2):
        steps.mark(nc.vector.tensor_tensor(R.onehot[:, k], R.onehot[:, k], over_last(R.weight[:, k, :], EXPERTS), ALU.mult))
    steps.settle()
    if scale != 1.0:
        steps.mark(nc.vector.tensor_scalar(R.onehot[:, 0], R.onehot[:, 0], scale, None, ALU.mult))
        steps.mark(nc.vector.tensor_scalar(R.onehot[:, 1], R.onehot[:, 1], scale, None, ALU.mult))
        steps.settle()
    nc.vector.tensor_tensor(out, R.onehot[:, 0], R.onehot[:, 1], ALU.add).then_inc(done, 1)


def softmax_weights(nc, steps, dve, R, exp_ready):
    dve.wait_ge(exp_ready, 1)
    steps.mark(nc.vector.tensor_scalar(R.weight[:, 0, :], R.gap, 1.0, None, ALU.add))
    steps.settle()
    steps.mark(nc.vector.reciprocal(R.weight[:, 0, :], R.weight[:, 0, :]))
    steps.settle()
    steps.mark(nc.vector.tensor_tensor(R.weight[:, 1, :], R.gap, R.weight[:, 0, :], ALU.mult))
    steps.settle()


class Routing:

    def __init__(self, take, priority):
        self.scores = take(B * EXPERTS).rearrange("p (b e) -> p b e", b=B)
        self.onehot = take(2 * B * EXPERTS).rearrange("p (k b e) -> p k b e", k=2, b=B)
        self.top = take(2 * B).rearrange("p (k b) -> p k b", k=2)
        self.weight = take(2 * B).rearrange("p (k b) -> p k b", k=2)
        self.tie = take(B)
        self.gap = take(B)
        self.priority = priority


class Arena:

    def __init__(self, T, at=0):
        self.T, self.at = T, at

    def __call__(self, cols, dt=F32):
        v = self.T.view(self.at, cols)
        self.at += cols
        assert self.at <= ARENA, self.at
        return v if dt == F32 else v.bitcast(dt)


def turn_xn(nc, pe, T, xn_ready, xn_turned):
    for c in range(DC):
        for b in range(B):
            if c == 0:
                pe.wait_ge(xn_ready, b + 1)
            t = nc.tensor.transpose(T.PS[:, 2 * c + b // 4, (b % 4) * P:(b % 4 + 1) * P],
                                    T.XN[:, b, c * P:(c + 1) * P], T.ident[:, :])
            if b % 4 == 3:
                t.then_inc(xn_turned, 1)


def copy_xnT(nc, act, T, xn_turned, xnT_ready):
    for k in range(2 * DC):
        act.wait_ge(xn_turned, k + 1)
        nc.scalar.activation(T.XNT[:, k // 2, (k % 2) * HALF:(k % 2 + 1) * HALF], T.PS[:, k, :],
                             ACT.Copy).then_inc(xnT_ready, 1)


def l1_ffn(nc, T, sem):
    step, var_ready, rstd_ready, xn_ready, xn_turned, xnT_ready = map(sem, ("l1f_step", "l1f_var", "l1f_rstd", "l1f_xn", "l1f_xn_turned", "l1f_xnT"))
    w_in, low_mm, gap_ready, exp_ready, cw_ready = map(sem, ("l1f_w_in", "l1f_low_mm", "l1f_gap", "l1f_exp", "l1f_cw"))
    t_ready, t_turned, tT_ready, out_mm, x_done = map(sem, ("l1f_t", "l1f_t_turned", "l1f_tT", "l1f_out_mm", "l1f_x"))
    X, PS = T.X, T.PS
    ER = EXPERTS * RANK
    LOW = ER + EXPERTS
    take = Arena(T)
    WT = take(DC * D).rearrange("p (c o) -> p c o", c=DC)
    LOWT = take(DC * LOW).rearrange("p (c o) -> p c o", c=DC)
    BT = take(D)
    CW = take(B * EXPERTS).rearrange("p (b e) -> p b e", b=B)
    TW = take(B * ER).rearrange("p (b e r) -> p b e r", b=B, e=EXPERTS)
    TWT = take(N)
    R = Routing(take, T.priority[:, :])

    def low(b):
        return PS[:, 4 + b // 3, (b % 3) * LOW:(b % 3 + 1) * LOW]

    with nc.Block() as block:

        @block.sync
        def _(sp):
            sp.dma_start(LOWT[:, :, :], T.dram["l1f_low"].rearrange("(c p) o -> p c o", c=DC)).then_inc(w_in, 16)
            sp.dma_start(WT[:, :, :], T.dram["l1f_w"].rearrange("(c p) o -> p c o", c=DC)).then_inc(w_in, 16)
            sp.dma_start(BT[:, :], T.dram["l1f_b"]).then_inc(w_in, 16)

        @block.gpsimd
        def _(pool):
            rstd_on_pool(nc, pool, T, var_ready, rstd_ready)

        @block.tensor
        def _(pe):
            turn_xn(nc, pe, T, xn_ready, xn_turned)
            pe.wait_ge(w_in, 48)
            pe.wait_ge(xnT_ready, 4)
            for b in range(B):
                for c in range(DC):
                    t = nc.tensor.matmul(low(b), T.XNT[:, c, b * S:(b + 1) * S], LOWT[:, c, :], start=(c == 0), stop=(c == DC - 1))
            t.then_inc(low_mm, 1)
            for b in range(B):
                pe.wait_ge(t_ready, b + 1)
                t = nc.tensor.transpose(PS[:, b // 4, (b % 4) * P:(b % 4 + 1) * P], TW[:, b].rearrange("p e r -> p (e r)"), T.ident[:, :])
                if b % 4 == 3:
                    t.then_inc(t_turned, 1)
            for b in range(B):
                if b % 4 == 0:
                    pe.wait_ge(tT_ready, b // 4 + 1)
                out = PS[:, 4 + b // 2, (b % 2) * D:(b % 2 + 1) * D]
                for c in range(DC):
                    nc.tensor.matmul(out, T.XNT[:, c, b * S:(b + 1) * S], WT[:, c, :], start=(c == 0), stop=False)
                t = nc.tensor.matmul(out, TWT[:, b * S:(b + 1) * S], BT[:, :], start=False, stop=True)
                if b % 2:
                    t.then_inc(out_mm, 1)

        @block.scalar
        def _(act):
            copy_xnT(nc, act, T, xn_turned, xnT_ready)
            act.wait_ge(gap_ready, 1)
            nc.scalar.activation(R.gap, R.gap, ACT.Exp).then_inc(exp_ready, 1)
            for k in range(2):
                act.wait_ge(t_turned, k + 1)
                nc.scalar.activation(TWT[:, k * HALF:(k + 1) * HALF], PS[:, k, :], ACT.Copy).then_inc(tT_ready, 1)

        @block.vector
        def _(dve):
            steps = Steps(dve, step)
            row_stats(nc, steps, T, lambda b: X[:, b, :], LN_EPS, var_ready)
            dve.wait_ge(rstd_ready, 1)
            normalise(nc, T, lambda b: X[:, b, :], lambda b: T.XN[:, b, :], xn_ready)
            dve.wait_ge(low_mm, 1)
            for b in range(B):
                steps.mark(nc.vector.tensor_copy(R.scores[:, b, :], low(b)[:, ER:LOW]))
            steps.settle()
            top_two(nc, steps, R)
            nc.vector.tensor_tensor(R.gap, R.top[:, 1, :], R.top[:, 0, :], ALU.subtract).then_inc(gap_ready, 1)
            softmax_weights(nc, steps, dve, R, exp_ready)
            combine(nc, steps, R, CW[:, :, :], LORA_ALPHA, cw_ready)
            dve.wait_ge(cw_ready, 1)
            for b in range(B):
                nc.vector.tensor_tensor(TW[:, b], low(b)[:, 0:ER].rearrange("p (e r) -> p e r", e=EXPERTS),
                                        over_last(CW[:, b, :], RANK), ALU.mult).then_inc(t_ready, 1)
            for k in range(4):
                dve.wait_ge(out_mm, k + 1)
                nc.vector.tensor_tensor(X[:, 2 * k:2 * k + 2, :], X[:, 2 * k:2 * k + 2, :],
                                        PS[:, 4 + k, :].rearrange("p (b d) -> p b d", b=2), ALU.add).then_inc(x_done, 1)
            dve.wait_ge(x_done, 4)


L2_TERMS = [(i, j) for i in range(PARTS) for j in range(PARTS)]


def l2_attention(nc, T, sem):
    step, var_ready, rstd_ready, xn_ready, xn_turned, xnT_ready = map(sem, ("l2a_step", "l2a_var", "l2a_rstd", "l2a_xn", "l2a_xn_turned", "l2a_xnT"))
    w_in, proj_mm, squared, v_ready, proj_read = map(sem, ("l2a_w_in", "l2a_proj_mm", "l2a_squared", "l2a_v", "l2a_proj_read"))
    ms_ready, rms_ready, qk_ready, qk_turned, whole_ready, split_done = map(sem, ("l2a_ms", "l2a_rms", "l2a_qk", "l2a_turned", "l2a_whole", "l2a_split"))
    written = [sem("l2a_k_written"), sem("l2a_q_written")]
    BUFS = 4
    stack_in = [sem(f"l2a_stack_in{n}") for n in range(BUFS)]
    score_mm, exp_ready, pv_mm, att_ready, att_turned, x_done = map(sem, ("l2a_score_mm", "l2a_exp", "l2a_pv_mm", "l2a_att", "l2a_att_turned", "l2a_x"))
    X, PS = T.X, T.PS
    HH = L2_H // 2
    PITCH = P + L2_HD
    ROWS = PARTS * PARTS * L2_HD
    take = Arena(T)
    WQ = take(DC * D).rearrange("p (c o) -> p c o", c=DC)
    WKV = take(DC * 2 * D).rearrange("p (c o) -> p c o", c=DC)
    KN = take(B * D).rearrange("p (b d) -> p b d", b=B)
    QN = take(B * D).rearrange("p (b d) -> p b d", b=B)
    SQ = take(2 * D).rearrange("p (r d) -> p r d", r=2)
    MS = take(2 * B * L2_H).rearrange("p (k b h) -> p k b h", k=2, b=B)
    RMS = take(2 * B * L2_H).rearrange("p (k b h) -> p k b h", k=2, b=B)
    parts = [[take(DC * N // 2, BF16).rearrange("p (c n) -> p c n", c=DC) for _ in range(PARTS)] for _ in range(2)]
    whole = take(DC * N).rearrange("p (c n) -> p c n", c=DC)
    KS = [take(L2_H * S // 2, BF16).rearrange("p (h t) -> p h t", h=L2_H) for _ in range(BUFS)]
    QS = [take(L2_H * S // 2, BF16).rearrange("p (h t) -> p h t", h=L2_H) for _ in range(BUFS)]
    padded = take((2 * B + 1) * 4 * PITCH)
    VZ = [padded[:, n * 4 * PITCH:(n + 1) * 4 * PITCH] for n in range(2 * B)]
    OZ = padded[:, 2 * B * 4 * PITCH:]
    E = KN[:, :, :].rearrange("p b d -> p (b d)").rearrange("p (s h n) -> p s h n", s=2, h=8)
    REC = take(2 * D).rearrange("p (r d) -> p r d", r=2)
    ATT = take(2 * D).rearrange("p (r d) -> p r d", r=2)
    UNITS = 4
    SCALE = float(L2_HD) ** -0.5

    with nc.Block() as block:

        @block.sync
        def _(sp):
            sp.dma_start(WKV[:, :, :], T.dram["l2_wkv"].rearrange("(c p) o -> p c o", c=DC)).then_inc(w_in, 16)
            sp.dma_start(WQ[:, :, :], T.dram["l2_wq"].rearrange("(c p) o -> p c o", c=DC)).then_inc(w_in, 16)
            for side in range(2):
                sp.wait_ge(split_done, 4 * side + 4)
                for m, pair in enumerate(L2_TERMS):
                    for c in range(DC):
                        sp.dma_start(T.scr_l2[side, m, :, c * HH:(c + 1) * HH, :].rearrange("d h t -> h d t"),
                                     parts[side][pair[1 - side]][:, c, :]).then_inc(written[side], 16)
            for side in range(2):
                sp.wait_ge(written[side], 16 * DC * len(L2_TERMS))
            for b in range(B):
                if b >= BUFS:
                    sp.wait_ge(score_mm, UNITS * (b - BUFS + 1))
                for side, stack in ((0, KS), (1, QS)):
                    sp.dma_start(stack[b % BUFS][0:ROWS],
                                 T.scr_l2[side, :, :, :, b * S:(b + 1) * S].rearrange("m d h t -> (m d) h t")).then_inc(stack_in[b % BUFS], 16)

        @block.gpsimd
        def _(pool):
            for side in range(2):
                if side:
                    rstd_on_pool(nc, pool, T, var_ready, rstd_ready)
                pool.wait_ge(ms_ready, side + 1)
                nc.gpsimd.tensor_tensor(RMS[:, side].rearrange("p b h -> p (b h)"), MS[:, side].rearrange("p b h -> p (b h)"),
                                        T.minus_half[:, 0:B * L2_H], ALU.pow).then_inc(rms_ready, 1)

        @block.tensor
        def _(pe):
            pe.wait_ge(w_in, 32)
            for b in range(B):
                for c in range(DC):
                    t = nc.tensor.matmul(PS[:, b, :], T.CTXT[:, c, b * S:(b + 1) * S], WKV[:, c, :], start=(c == 0), stop=(c == DC - 1))
                t.then_inc(proj_mm, 1)
            pe.wait_ge(qk_ready, B)
            for c in range(DC):
                for b in range(B):
                    t = nc.tensor.transpose(PS[:, 4 + 2 * c + b // 4, (b % 4) * P:(b % 4 + 1) * P], KN[:, b, c * P:(c + 1) * P], T.ident[:, :])
                    if b % 4 == 3:
                        t.then_inc(qk_turned, 1)
            turn_xn(nc, pe, T, xn_ready, xn_turned)
            pe.wait_ge(xnT_ready, 4)
            for b in range(B):
                for c in range(DC):
                    t = nc.tensor.matmul(PS[:, b // 2, (b % 2) * D:(b % 2 + 1) * D], T.XNT[:, c, b * S:(b + 1) * S], WQ[:, c, :],
                                         start=(c == 0), stop=(c == DC - 1))
                if b % 2:
                    t.then_inc(proj_mm, 1)
            pe.wait_ge(whole_ready, 4)
            for c in range(DC):
                for b in range(B):
                    if c == 0:
                        pe.wait_ge(qk_ready, B + b + 1)
                    t = nc.tensor.transpose(PS[:, 4 + 2 * c + b // 4, (b % 4) * P:(b % 4 + 1) * P], QN[:, b, c * P:(c + 1) * P], T.ident[:, :])
                    if b % 4 == 3:
                        t.then_inc(qk_turned, 1)
            pe.wait_ge(whole_ready, 8)

            def scores(n):
                b, u = n // UNITS, n % UNITS
                c, g0 = u // 2, 2 * (u % 2)
                if u == 0:
                    pe.wait_ge(stack_in[b % BUFS], 32 * (b // BUFS + 1))
                if n >= 2:
                    pe.wait_ge(exp_ready, n - 1)
                for k in range(8):
                    h = HH * c + 4 * (k % 4) + g0 + k // 4
                    t = nc.tensor.matmul(PS[:, 2 * (n % 2) + k // 4, (k % 4) * S:(k % 4 + 1) * S],
                                         KS[b % BUFS][0:ROWS, h, :], QS[b % BUFS][0:ROWS, h, :], start=True, stop=True)
                t.then_inc(score_mm, 1)

            def weigh(n):
                b, u = n // UNITS, n % UNITS
                c, g0 = u // 2, 2 * (u % 2)
                pe.wait_ge(exp_ready, n + 1)
                if u == 0 and b:
                    pe.wait_ge(att_ready, b)
                for bank, tile in ((4, VZ[2 * b + c]), (5, OZ)):
                    for k in range(8):
                        g, j = g0 + k // 4, k % 4
                        t = nc.tensor.matmul(PS[32 * j:32 * j + 32, bank, c * S:(c + 1) * S],
                                             tile[:, g * P + 32 * j:g * P + 32 * j + 32], E[:, n % 2, k, :],
                                             start=(g == 0), stop=(g == 3))
                t.then_inc(pv_mm, 1)

            def turn_back(b):
                pe.wait_ge(att_ready, b + 1)
                if b >= 2:
                    pe.wait_ge(x_done, b - 1)
                for c in range(DC):
                    t = nc.tensor.transpose(PS[:, 6 + b % 2, c * P:(c + 1) * P], ATT[:, b % 2, c * S:(c + 1) * S], T.ident[:, :])
                t.then_inc(att_turned, 1)

            for n in range(B * UNITS):
                scores(n)
                if n:
                    weigh(n - 1)
                if n % UNITS == 2 and n > UNITS:
                    turn_back(n // UNITS - 1)
            weigh(B * UNITS - 1)
            turn_back(B - 1)

        @block.scalar
        def _(act):
            for b in range(B):
                act.wait_ge(proj_mm, b + 1)
                if b >= 2:
                    act.wait_ge(proj_read, b - 1)
                nc.scalar.activation(SQ[:, b % 2, :], PS[:, b, 0:D], ACT.Square).then_inc(squared, 1)
            for k in range(4):
                act.wait_ge(qk_turned, k + 1)
                cols = slice((k % 2) * HALF, (k % 2 + 1) * HALF)
                nc.scalar.activation(parts[0][0][:, k // 2, cols], PS[:, 4 + k, :], ACT.Copy)
                nc.scalar.activation(whole[:, k // 2, cols], PS[:, 4 + k, :], ACT.Copy).then_inc(whole_ready, 1)
            copy_xnT(nc, act, T, xn_turned, xnT_ready)
            for b in range(B):
                act.wait_ge(proj_mm, B + b // 2 + 1)
                act.wait_ge(proj_read, B + b - 1)
                nc.scalar.activation(SQ[:, b % 2, :], PS[:, b // 2, (b % 2) * D:(b % 2 + 1) * D], ACT.Square).then_inc(squared, 1)
            for k in range(4):
                act.wait_ge(qk_turned, 4 + k + 1)
                act.wait_ge(split_done, k + 1)
                cols = slice((k % 2) * HALF, (k % 2 + 1) * HALF)
                nc.scalar.activation(parts[1][0][:, k // 2, cols], PS[:, 4 + k, :], ACT.Copy)
                nc.scalar.activation(whole[:, k // 2, cols], PS[:, 4 + k, :], ACT.Copy).then_inc(whole_ready, 1)
            for n in range(B * UNITS):
                act.wait_ge(score_mm, n + 1)
                if n >= 2:
                    act.wait_ge(pv_mm, n - 1)
                nc.scalar.activation(E[:, n % 2].rearrange("p (a h) n -> p a (h n)", a=2), PS[:, 2 * (n % 2):2 * (n % 2) + 2, :],
                                     ACT.Exp, scale=SCALE).then_inc(exp_ready, 1)

        @block.vector
        def _(dve):
            steps = Steps(dve, step)
            steps.mark(nc.vector.memset(padded[:, :], 0.0))
            steps.settle()
            ones_at = OZ[:, :].rearrange("p (g x) -> p g x", x=PITCH)[:, :, 0:P].rearrange("p g (j r) -> p g j r", r=32)
            for g in range(4):
                steps.mark(nc.vector.memset(ones_at[:, g, :, 0:L2_HD], 1.0))

            def mean_squares(side):
                for b in range(B):
                    dve.wait_ge(squared, B * side + b + 1)
                    nc.vector.tensor_reduce(MS[:, side, b, :], SQ[:, b % 2, :].rearrange("p (h d) -> p h d", h=L2_H),
                                            AX.X, ALU.add).then_inc(proj_read, 1)
                dve.wait_ge(proj_read, B * (side + 1))
                nc.vector.tensor_scalar(MS[:, side], MS[:, side], 1.0 / L2_HD, RMS_EPS, ALU.mult, ALU.add).then_inc(ms_ready, 1)

            def unit_heads(side, target, source):
                dve.wait_ge(rms_ready, side + 1)
                for b in range(B):
                    nc.vector.tensor_tensor(target[:, b, :].rearrange("p (h d) -> p h d", h=L2_H),
                                            source(b).rearrange("p (h d) -> p h d", h=L2_H),
                                            over_last(RMS[:, side, b, :], L2_HD), ALU.mult).then_inc(qk_ready, 1)

            def split(side):
                for k in range(4):
                    dve.wait_ge(whole_ready, 4 * side + k + 1)
                    cols = slice((k % 2) * HALF, (k % 2 + 1) * HALF)
                    split_rest(nc, steps, whole[:, k // 2, cols], *(parts[side][i][:, k // 2, cols] for i in range(PARTS)), split_done)

            mean_squares(0)
            for b in range(B):
                for c in range(DC):
                    target = VZ[2 * b + c][:, :].rearrange("p (g x) -> p g x", x=PITCH)[:, :, 0:P].rearrange("p g (j r) -> p g j r", r=32)[:, :, :, 0:L2_HD]
                    nc.vector.tensor_copy(target, PS[:, b, D + c * P:D + (c + 1) * P].rearrange("p (j g d) -> p g j d", j=4, g=4)).then_inc(v_ready, 1)
            unit_heads(0, KN, lambda b: PS[:, b, 0:D])
            row_stats(nc, steps, T, lambda b: X[:, b, :], LN_EPS, var_ready)
            dve.wait_ge(rstd_ready, 1)
            normalise(nc, T, lambda b: X[:, b, :], lambda b: T.XN[:, b, :], xn_ready)
            split(0)
            mean_squares(1)
            unit_heads(1, QN, lambda b: PS[:, b // 2, (b % 2) * D:(b % 2 + 1) * D])
            split(1)

            def attended(b):
                dve.wait_ge(pv_mm, UNITS * (b + 1))
                r = b % 2
                if b >= 2:
                    dve.wait_ge(att_turned, b - 1)
                steps.mark(nc.vector.reciprocal(REC[:, r, :], PS[:, 5, 0:D]))
                steps.settle()
                nc.vector.tensor_tensor(ATT[:, r, :], PS[:, 4, 0:D], REC[:, r, :], ALU.mult).then_inc(att_ready, 1)

            def add(b):
                dve.wait_ge(att_turned, b + 1)
                nc.vector.tensor_tensor(X[:, b, :], X[:, b, :], PS[:, 6 + b % 2, 0:D], ALU.add).then_inc(x_done, 1)

            for b in range(B):
                attended(b)
                if b:
                    add(b - 1)
            add(B - 1)
            dve.wait_ge(x_done, B)


def moe_ffn(nc, T, sem, name, n_experts, chunks, width, sigmoid_router, shared_gate, d_gate, d_up, d_down, d_router):
    s = lambda n: sem(f"{name}_{n}")
    step, var_ready, rstd_ready, xn_ready, xn_turned, xnT_ready = map(s, ("step", "var", "rstd", "xn", "xn_turned", "xnT"))
    router_in, logit_mm, act_in, act_out, cw_ready = map(s, ("router_in", "logit_mm", "act_in", "act_out", "cw"))
    weights_in = [s("weights_in0"), s("weights_in1")]
    up_mm, silu_ready, h_ready, down_mm, x_done = map(s, ("up_mm", "silu", "h", "down_mm", "x"))
    X, PS = T.X, T.PS
    cols = chunks * width
    n_router = EXPERTS + (1 if shared_gate else 0)
    take = Arena(T)
    ROUTER = take(DC * n_router).rearrange("p (c e) -> p c e", c=DC)
    CW = take(B * n_experts).rearrange("p (b e) -> p b e", b=B)
    LOGITS = take(B * n_router).rearrange("p (b e) -> p b e", b=B)
    R = Routing(take, T.priority[:, :])
    WG = [take(DC * cols).rearrange("p (c i) -> p c i", c=DC) for _ in range(2)]
    WU = [take(DC * cols).rearrange("p (c i) -> p c i", c=DC) for _ in range(2)]
    WD = [take(chunks * D).rearrange("p (k d) -> p k d", k=chunks) for _ in range(2)]
    SILU = take(2 * HALF).rearrange("p (r n) -> p r n", r=2)
    HT = [take(chunks * HALF).rearrange("p (k n) -> p k n", k=chunks) for _ in range(2)]
    PIECES = 2 * n_experts

    with nc.Block() as block:

        @block.sync
        def _(sp):
            sp.dma_start(ROUTER[:, :, :], d_router.rearrange("(c p) e -> p c e", c=DC)).then_inc(router_in, 16)
            for e in range(n_experts):
                if e >= 2:
                    sp.wait_ge(down_mm, 4 * (e - 1))
                sp.dma_start(WG[e % 2][:, :, :], d_gate[e].rearrange("(c p) i -> p c i", c=DC)).then_inc(weights_in[e % 2], 16)
                sp.dma_start(WU[e % 2][:, :, :], d_up[e].rearrange("(c p) i -> p c i", c=DC)).then_inc(weights_in[e % 2], 16)
                sp.dma_start(WD[e % 2][0:width], d_down[e].rearrange("(k p) d -> p k d", k=chunks)).then_inc(weights_in[e % 2], 16)

        @block.gpsimd
        def _(pool):
            rstd_on_pool(nc, pool, T, var_ready, rstd_ready)

        @block.tensor
        def _(pe):
            turn_xn(nc, pe, T, xn_ready, xn_turned)
            pe.wait_ge(xnT_ready, 4)
            pe.wait_ge(router_in, 16)
            for b in range(B):
                for c in range(DC):
                    t = nc.tensor.matmul(PS[:, 7, b * n_router:(b + 1) * n_router], T.XNT[:, c, b * S:(b + 1) * S], ROUTER[:, c, :],
                                         start=(c == 0), stop=(c == DC - 1))
            t.then_inc(logit_mm, 1)

            def up(p, k):
                e, g = p // 2, p % 2
                n = chunks * p + k
                if g == 0 and k == 0:
                    pe.wait_ge(weights_in[e % 2], 48 * (e // 2 + 1))
                if n >= 2:
                    pe.wait_ge(h_ready, n - 1)
                for bank, w in ((0, WG[e % 2]), (1, WU[e % 2])):
                    for c in range(DC):
                        t = nc.tensor.matmul(PS[0:width, 2 * (n % 2) + bank, :], w[:, c, k * width:(k + 1) * width],
                                             T.XNT[:, c, g * HALF:(g + 1) * HALF], start=(c == 0), stop=(c == DC - 1))
                t.then_inc(up_mm, 1)

            def down(p):
                e = p // 2
                pe.wait_ge(h_ready, chunks * (p + 1))
                for q in range(2):
                    if 2 * p + q >= 4:
                        pe.wait_ge(x_done, 2 * (2 * p + q) - 6)
                    for b in (2 * q, 2 * q + 1):
                        for k in range(chunks):
                            t = nc.tensor.matmul(PS[:, 4 + 2 * (p % 2) + q, (b % 2) * D:(b % 2 + 1) * D],
                                                 HT[p % 2][0:width, k, b * S:(b + 1) * S], WD[e % 2][0:width, k, :],
                                                 start=(k == 0), stop=(k == chunks - 1))
                    t.then_inc(down_mm, 1)

            pe.wait_ge(cw_ready, 1)
            for p in range(PIECES):
                for k in range(chunks):
                    up(p, k)
                    if k == 0 and p:
                        down(p - 1)
            down(PIECES - 1)

        @block.scalar
        def _(act):
            copy_xnT(nc, act, T, xn_turned, xnT_ready)
            act.wait_ge(act_in, 1)
            if sigmoid_router:
                nc.scalar.activation(R.scores, LOGITS[:, :, :], ACT.Exp, scale=-1.0).then_inc(act_out, 1)
            else:
                nc.scalar.activation(R.gap, R.gap, ACT.Exp).then_inc(act_out, 1)
            if shared_gate:
                nc.scalar.activation(LOGITS[:, :, EXPERTS], LOGITS[:, :, EXPERTS], ACT.Exp, scale=-1.0).then_inc(act_out, 1)
            for n in range(PIECES * chunks):
                act.wait_ge(up_mm, n + 1)
                if n >= 2:
                    act.wait_ge(h_ready, n - 1)
                nc.scalar.activation(SILU[0:width, n % 2, :], PS[0:width, 2 * (n % 2), :], ACT.Silu).then_inc(silu_ready, 1)

        @block.vector
        def _(dve):
            steps = Steps(dve, step)
            row_stats(nc, steps, T, lambda b: X[:, b, :], LN_EPS, var_ready)
            dve.wait_ge(rstd_ready, 1)
            normalise(nc, T, lambda b: X[:, b, :], lambda b: T.XN[:, b, :], xn_ready)
            dve.wait_ge(logit_mm, 1)
            steps.mark(nc.vector.tensor_copy(LOGITS[:, :, :], PS[:, 7, 0:B * n_router].rearrange("p (b e) -> p b e", b=B)))
            steps.settle()
            if sigmoid_router:
                nc.vector.tensor_scalar(LOGITS[:, :, :], LOGITS[:, :, :], -87.0, None, ALU.max).then_inc(act_in, 1)
                dve.wait_ge(act_out, 1)
                steps.mark(nc.vector.tensor_scalar(R.scores, R.scores, 1.0, None, ALU.add))
                steps.settle()
                steps.mark(nc.vector.reciprocal(R.scores, R.scores))
                steps.settle()
                top_two(nc, steps, R)
                steps.mark(nc.vector.tensor_tensor(R.tie, R.top[:, 0, :], R.top[:, 1, :], ALU.add))
                steps.settle()
                steps.mark(nc.vector.reciprocal(R.tie, R.tie))
                steps.settle()
                for k in range(2):
                    steps.mark(nc.vector.tensor_tensor(R.weight[:, k, :], R.top[:, k, :], R.tie, ALU.mult))
                steps.settle()
                steps.mark(nc.vector.memset(CW[:, :, EXPERTS:], 1.0))
            else:
                steps.mark(nc.vector.tensor_copy(R.scores, LOGITS[:, :, 0:EXPERTS]))
                steps.settle()
                top_two(nc, steps, R)
                nc.vector.tensor_tensor(R.gap, R.top[:, 1, :], R.top[:, 0, :], ALU.subtract).then_inc(act_in, 1)
                softmax_weights(nc, steps, dve, R, act_out)
                dve.wait_ge(act_out, 2)
                steps.mark(nc.vector.tensor_scalar(LOGITS[:, :, EXPERTS], LOGITS[:, :, EXPERTS], 1.0, None, ALU.add))
                steps.settle()
                for k in range(EXPERTS, n_experts):
                    steps.mark(nc.vector.reciprocal(CW[:, :, k], LOGITS[:, :, EXPERTS]))
            steps.settle()
            combine(nc, steps, R, CW[:, :, 0:EXPERTS], 1.0, cw_ready)
            dve.wait_ge(cw_ready, 1)

            def hidden(p, k):
                n = chunks * p + k
                if k == 0 and p >= 2:
                    dve.wait_ge(down_mm, 2 * (p - 1))
                dve.wait_ge(silu_ready, n + 1)
                nc.vector.tensor_tensor(HT[p % 2][0:width, k, :], SILU[0:width, n % 2, :],
                                        PS[0:width, 2 * (n % 2) + 1, :], ALU.mult).then_inc(h_ready, 1)

            def add(p):
                e, g = p // 2, p % 2
                for q in range(2):
                    dve.wait_ge(down_mm, 2 * p + q + 1)
                    for b in (4 * g + 2 * q, 4 * g + 2 * q + 1):
                        nc.vector.scalar_tensor_tensor(out=X[:, b, :], in0=PS[:, 4 + 2 * (p % 2) + q, (b % 2) * D:(b % 2 + 1) * D],
                                                       scalar=CW[:, b, e:e + 1], in1=X[:, b, :],
                                                       op0=ALU.mult, op1=ALU.add).then_inc(x_done, 1)

            for p in range(PIECES):
                for k in range(chunks):
                    hidden(p, k)
                    if k == 1 and p:
                        add(p - 1)
            add(PIECES - 1)
            dve.wait_ge(x_done, 4 * PIECES)


def l2_ffn(nc, T, sem):
    moe_ffn(nc, T, sem, "l2f", EXPERTS + L2_SHARED, L2_I // P, P, True, False,
            T.dram["l2f_gate"], T.dram["l2f_up"], T.dram["l2f_down"], T.dram["l2f_router"])


def l3_ffn(nc, T, sem):
    moe_ffn(nc, T, sem, "l3f", EXPERTS + L3_SI // L3_I, 2, L3_I // 2, False, True,
            T.dram["l3f_gate"], T.dram["l3f_up"], T.dram["l3f_down"], T.dram["l3f_router"])


L3_TERMS = [(0, 0), (0, 1), (1, 0), (1, 1), (0, 2), (2, 0)]


def l3_attention(nc, T, sem):
    step, var_ready, rstd_ready, xn_ready, xn_turned, xnT_ready = map(sem, ("l3a_step", "l3a_var", "l3a_rstd", "l3a_xn", "l3a_xn_turned", "l3a_xnT"))
    w_in, small_in, proj_mm, copied, v_mm, v_ready, split_done = map(sem, ("l3a_w_in", "l3a_small_in", "l3a_proj_mm", "l3a_copied", "l3a_v_mm", "l3a_v", "l3a_split"))
    written = [sem("l3a_k_written"), sem("l3a_q_written")]
    BUFS = 2
    stack_in = [sem(f"l3a_stack_in{n}") for n in range(BUFS)]
    score_mm, clip_ready, exp_ready, pv_mm, att_ready, out_mm, delta_ready, x_done = map(sem, ("l3a_score_mm", "l3a_clip", "l3a_exp", "l3a_pv_mm", "l3a_att", "l3a_out_mm", "l3a_delta", "l3a_x"))
    att_freed = sem("l3a_att_freed")
    X, PS = T.X, T.PS
    HH = L3_H // 2
    PITCH = P + L3_HD
    ROWS = len(L3_TERMS) * L3_HD
    NG = 2
    SCALE = float(L3_HD) ** -0.5
    LIM = SCORE_LIM / SCALE
    take = Arena(T)
    WQ, WK, WV, WO = (take(DC * D).rearrange("p (c o) -> p c o", c=DC) for _ in range(4))
    BQK = take(2 * DC).rearrange("p (w c) -> p w c", w=2)
    ROWB = take(4 * D).rearrange("p (w d) -> p w d", w=4)
    MASK = take(B, I32)
    UPPER = take(B)
    RS = take(1)
    parts = [[take(DC * N // 2, BF16).rearrange("p (c n) -> p c n", c=DC) for _ in range(PARTS)] for _ in range(2)]
    whole = [take(DC * N).rearrange("p (c n) -> p c n", c=DC) for _ in range(2)]
    STK = [[take(L3_H * S // 2, BF16).rearrange("p (h t) -> p h t", h=L3_H) for _ in range(BUFS)] for _ in range(2)]
    padded = take((2 * B + 1) * NG * PITCH)
    VZ = [padded[:, n * NG * PITCH:(n + 1) * NG * PITCH] for n in range(2 * B)]
    OZ = padded[:, 2 * B * NG * PITCH:]
    VT = take(2 * D).rearrange("p (r o) -> p r o", r=2)
    CLIP = take(2 * 8 * S).rearrange("p (s h n) -> p s h n", s=2, h=8)
    E = take(2 * 8 * S).rearrange("p (s h n) -> p s h n", s=2, h=8)
    REC = take(2 * D).rearrange("p (r d) -> p r d", r=2)
    CT = take(DC * N).rearrange("p (c n) -> p c n", c=DC)
    DELTA = take(B * D).rearrange("p (b d) -> p b d", b=B)
    UNITS = 2

    with nc.Block() as block:

        @block.sync
        def _(sp):
            for w, name in ((WK, "k"), (WV, "v"), (WQ, "q"), (WO, "o")):
                sp.dma_start(w[:, :, :], T.dram["l3_w" + name].rearrange("(c p) o -> p c o", c=DC)).then_inc(w_in, 16)
            sp.dma_start(BQK[:, :, :], T.dram["l3_bqk"].rearrange("p (w c) -> p w c", w=2)).then_inc(small_in, 16)
            sp.dma_start(ROWB[:, :, :], T.dram["l3_rows"].unsqueeze(0).to_broadcast([P, 4, D])).then_inc(small_in, 16)
            sp.dma_start(MASK[:, :], T.dram["l3_mask"]).then_inc(small_in, 16)
            sp.dma_start(RS[:, :], T.dram["l3_rs"].unsqueeze(0).to_broadcast([P, 1])).then_inc(small_in, 16)
            for side in range(2):
                sp.wait_ge(split_done, 4 * side + 4)
                for m, pair in enumerate(L3_TERMS):
                    for c in range(DC):
                        sp.dma_start(T.scr_l3[side, m, :, c * HH:(c + 1) * HH, :].rearrange("d h t -> h d t"),
                                     parts[side][pair[1 - side]][:, c, :]).then_inc(written[side], 16)
            for side in range(2):
                sp.wait_ge(written[side], 16 * DC * len(L3_TERMS))
            for b in range(B):
                if b >= BUFS:
                    sp.wait_ge(score_mm, UNITS * (b - BUFS + 1))
                for side in range(2):
                    sp.dma_start(STK[side][b % BUFS][0:ROWS],
                                 T.scr_l3[side, :, :, :, b * S:(b + 1) * S].rearrange("m d h t -> (m d) h t")).then_inc(stack_in[b % BUFS], 16)

        @block.gpsimd
        def _(pool):
            rstd_on_pool(nc, pool, T, var_ready, rstd_ready, 1)
            rstd_on_pool(nc, pool, T, var_ready, rstd_ready, 2)

        @block.tensor
        def _(pe):
            pe.wait_ge(w_in, 64)
            for k in range(4):
                for c in range(DC):
                    t = nc.tensor.matmul(PS[:, 4 + k, :], WK[:, c, (k // 2) * P:(k // 2 + 1) * P],
                                         T.CTXT[:, c, (k % 2) * HALF:(k % 2 + 1) * HALF], start=(c == 0), stop=(c == DC - 1))
                t.then_inc(proj_mm, 1)
            turn_xn(nc, pe, T, xn_ready, xn_turned)
            pe.wait_ge(xnT_ready, 4)
            for b in range(B):
                for c in range(DC):
                    t = nc.tensor.matmul(PS[:, b // 2, (b % 2) * D:(b % 2 + 1) * D], T.CTXT[:, c, b * S:(b + 1) * S], WV[:, c, :],
                                         start=(c == 0), stop=(c == DC - 1))
                if b % 2:
                    t.then_inc(v_mm, 1)
            for k in range(4):
                pe.wait_ge(copied, 2 * k + 2)
                for c in range(DC):
                    t = nc.tensor.matmul(PS[:, 4 + k, :], WQ[:, c, (k // 2) * P:(k // 2 + 1) * P],
                                         T.XNT[:, c, (k % 2) * HALF:(k % 2 + 1) * HALF], start=(c == 0), stop=(c == DC - 1))
                t.then_inc(proj_mm, 1)
            pe.wait_ge(v_ready, 2 * B)
            pe.wait_ge(copied, 16)

            def scores(n):
                b, c = n // UNITS, n % UNITS
                if c == 0:
                    pe.wait_ge(stack_in[b % BUFS], 32 * (b // BUFS + 1))
                if n >= 2:
                    pe.wait_ge(clip_ready, n - 1)
                for k in range(8):
                    h = HH * c + 2 * (k % 4) + k // 4
                    t = nc.tensor.matmul(PS[:, 2 * (n % 2) + k // 4, (k % 4) * S:(k % 4 + 1) * S],
                                         STK[0][b % BUFS][0:ROWS, h, :], STK[1][b % BUFS][0:ROWS, h, :], start=True, stop=True)
                t.then_inc(score_mm, 1)

            def weigh(n):
                b, c = n // UNITS, n % UNITS
                pe.wait_ge(exp_ready, n + 1)
                if c == 0 and b:
                    pe.wait_ge(att_ready, b)
                for bank, tile in ((4, VZ[2 * b + c]), (5, OZ)):
                    for k in range(8):
                        g, j = k // 4, k % 4
                        t = nc.tensor.matmul(PS[32 * j:32 * j + 32, bank, c * S:(c + 1) * S],
                                             tile[:, g * P + 32 * j:g * P + 32 * j + 32], E[:, n % 2, k, :],
                                             start=(g == 0), stop=(g == NG - 1))
                t.then_inc(pv_mm, 1)

            def project(b):
                pe.wait_ge(att_ready, b + 1)
                if b >= 2:
                    pe.wait_ge(delta_ready, b - 1)
                for c in range(DC):
                    t = nc.tensor.matmul(PS[:, 6 + b % 2, 0:D], CT[:, c, b * S:(b + 1) * S], WO[:, c, :],
                                         start=(c == 0), stop=(c == DC - 1))
                t.then_inc(out_mm, 1)

            for n in range(B * UNITS):
                scores(n)
                if n:
                    weigh(n - 1)
                if n % UNITS == 1 and n > UNITS:
                    project(n // UNITS - 1)
            weigh(B * UNITS - 1)
            project(B - 1)

        @block.scalar
        def _(act):
            def copies(side):
                for k in range(4):
                    act.wait_ge(proj_mm, 4 * side + k + 1)
                    cols = slice((k % 2) * HALF, (k % 2 + 1) * HALF)
                    for target in (parts[side][0], whole[side]):
                        nc.scalar.activation(target[:, k // 2, cols], PS[:, 4 + k, :], ACT.Identity,
                                             bias=BQK[:, 1 - side, k // 2:k // 2 + 1]).then_inc(copied, 1)

            act.wait_ge(small_in, 64)
            copies(0)
            copy_xnT(nc, act, T, xn_turned, xnT_ready)
            copies(1)
            for n in range(B * UNITS):
                act.wait_ge(clip_ready, n + 1)
                if n >= 2:
                    act.wait_ge(pv_mm, n - 1)
                nc.scalar.activation(E[:, n % 2], CLIP[:, n % 2], ACT.Exp, scale=SCALE).then_inc(exp_ready, 1)

        @block.vector
        def _(dve):
            steps = Steps(dve, step)
            row_stats(nc, steps, T, lambda b: X[:, b, :], LN_EPS, var_ready)
            steps.mark(nc.vector.memset(padded[:, :], 0.0))
            steps.settle()
            ones_at = OZ[:, :].rearrange("p (g x) -> p g x", x=PITCH)[:, :, 0:P].rearrange("p g (j r) -> p g j r", r=32)
            for g in range(NG):
                steps.mark(nc.vector.memset(ones_at[:, g, :, 0:L3_HD], 1.0))
            dve.wait_ge(rstd_ready, 1)
            normalise(nc, T, lambda b: X[:, b, :], lambda b: T.XN[:, b, :], xn_ready)
            dve.wait_ge(small_in, 64)
            steps.mark(nc.vector.tensor_copy(UPPER[:, :], MASK[:, :]))
            steps.mark(nc.vector.tensor_scalar(RS[:, :], RS[:, :], 0.0, RES_SCALE_MAX, ALU.max, ALU.min))
            steps.settle()
            steps.mark(nc.vector.tensor_scalar(UPPER[:, :], UPPER[:, :], 0.5, 2.0 * LIM, ALU.is_gt, ALU.mult))
            steps.settle()
            steps.mark(nc.vector.tensor_scalar(UPPER[:, :], UPPER[:, :], LIM, None, ALU.subtract))

            def split(side):
                for k in range(4):
                    dve.wait_ge(copied, 8 * side + 2 * k + 2)
                    cols = slice((k % 2) * HALF, (k % 2 + 1) * HALF)
                    split_rest(nc, steps, whole[side][:, k // 2, cols], *(parts[side][i][:, k // 2, cols] for i in range(PARTS)), split_done)

            split(0)
            for b in range(B):
                dve.wait_ge(v_mm, b // 2 + 1)
                steps.mark(nc.vector.tensor_tensor(VT[:, b % 2, :], PS[:, b // 2, (b % 2) * D:(b % 2 + 1) * D], ROWB[:, 0, :], ALU.add))
                steps.settle()
                for c in range(DC):
                    target = VZ[2 * b + c][:, :].rearrange("p (g x) -> p g x", x=PITCH)[:, :, 0:P].rearrange("p g (j r) -> p g j r", r=32)[:, :, :, 0:L3_HD]
                    nc.vector.tensor_copy(target, VT[:, b % 2, c * P:(c + 1) * P].rearrange("p (j g d) -> p g j d", j=4, g=NG)).then_inc(v_ready, 1)
            split(1)

            def clip(n):
                dve.wait_ge(score_mm, n + 1)
                if n >= 2:
                    dve.wait_ge(exp_ready, n - 1)
                nc.vector.tensor_scalar(CLIP[:, n % 2].rearrange("p (a h) n -> p a (h n)", a=2), PS[:, 2 * (n % 2):2 * (n % 2) + 2, :],
                                        -LIM, UPPER[:, n // UNITS:n // UNITS + 1], ALU.max, ALU.min).then_inc(clip_ready, 1)

            def attended(b):
                dve.wait_ge(pv_mm, UNITS * (b + 1))
                steps.mark(nc.vector.reciprocal(REC[:, b % 2, :], PS[:, 5, 0:D]))
                steps.settle()
                nc.vector.tensor_tensor(CT[:, :, b * S:(b + 1) * S], PS[:, 4, 0:D].rearrange("p (c n) -> p c n", c=DC),
                                        REC[:, b % 2, :].rearrange("p (c n) -> p c n", c=DC), ALU.mult).then_inc(att_ready, 1)

            def delta(b):
                dve.wait_ge(out_mm, b + 1)
                nc.vector.tensor_tensor(DELTA[:, b, :], PS[:, 6 + b % 2, 0:D], ROWB[:, 1, :], ALU.add).then_inc(delta_ready, 1)

            for n in range(B * UNITS):
                clip(n)
                if n % UNITS == 1 and n > UNITS:
                    attended(n // UNITS - 1)
                    if n // UNITS >= 2:
                        delta(n // UNITS - 2)
            attended(B - 1)
            delta(B - 2)
            delta(B - 1)
            dve.wait_ge(delta_ready, B)
            steps.mark(nc.vector.tensor_scalar(DELTA[:, :, :], DELTA[:, :, :], RS[:, 0:1], None, ALU.mult))
            steps.settle()
            row_stats(nc, steps, T, lambda b: DELTA[:, b, :], LN_EPS, var_ready)
            dve.wait_ge(rstd_ready, 2)
            for b in range(B):
                steps.mark(nc.vector.tensor_scalar(DELTA[:, b, :], DELTA[:, b, :], T.mv[:, b, 0:1], T.rstd[:, b:b + 1],
                                                   ALU.subtract, ALU.mult))
            steps.settle()
            steps.mark(nc.vector.tensor_tensor(DELTA[:, :, :], DELTA[:, :, :], over_batches(ROWB[:, 2, :]), ALU.mult))
            steps.settle()
            steps.mark(nc.vector.tensor_tensor(DELTA[:, :, :], DELTA[:, :, :], over_batches(ROWB[:, 3, :]), ALU.add))
            steps.settle()
            nc.vector.tensor_tensor(X[:, :, :], X[:, :, :], DELTA[:, :, :], ALU.add).then_inc(x_done, 1)
            dve.wait_ge(x_done, 1)


def more_tensors(T, sb, sem):
    T.scr_k = T.scratch("scr_k", [B, PARTS, L1_HD, L1_H, POS], BF16)
    T.scr_l2 = T.scratch("scr_l2", [2, PARTS * PARTS, L2_HD, L2_H, N], BF16)
    T.scr_l3 = T.scratch("scr_l3", [2, len(L3_TERMS), L3_HD, L3_H, N], BF16)
    T.scr_q = T.scratch("scr_q", [B, PARTS, L1_HD, L1_H, POS], BF16)


def more_arrays(a, out):
    out["mask"] = a["mask_Bx1x2048_fk1"]
    out["l1_w"] = np.stack([a["L1_xattn_W" + n].T for n in "qkv"], axis=1)
    out["l1_bqk"] = np.stack([a["L1_xattn_bq"], a["L1_xattn_bk"]], axis=1)
    out["l1_bv"] = a["L1_xattn_bv"]
    out["priority"] = np.arange(EXPERTS, 0, -1, dtype=np.float32)
    out["l1f_w"] = a["L1_ffn_weight"].T
    out["l1f_low"] = np.concatenate([a["L1_ffn_A_w"].reshape(EXPERTS * RANK, D).T, a["L1_ffn_gate_w"].T], axis=1)
    out["l1f_b"] = a["L1_ffn_B_w"].transpose(0, 2, 1).reshape(EXPERTS * RANK, D)
    kv = np.concatenate([a["L2_xattn_Wk"], a["L2_xattn_Wv"]], axis=0).T
    out["l2_wkv"] = np.concatenate([kv[:, 0::2], kv[:, 1::2]], axis=1)
    out["l2_wq"] = a["L2_xattn_Wq"].T
    out["l2f_gate"] = np.concatenate([a["L2_ffn_wg"], a["L2_ffn_sg"]]).transpose(0, 2, 1)
    out["l2f_up"] = np.concatenate([a["L2_ffn_wu"], a["L2_ffn_su"]]).transpose(0, 2, 1)
    out["l2f_down"] = np.concatenate([a["L2_ffn_wd"], a["L2_ffn_sd"]]).transpose(0, 2, 1)
    out["l2f_router"] = a["L2_ffn_w_router"].T
    for n in "qkvo":
        out["l3_w" + n] = a["L3_xattn_W" + n].T
    out["l3_bqk"] = np.stack([a["L3_xattn_bq"], a["L3_xattn_bk"]]).reshape(2 * DC, P).T
    out["l3_rows"] = np.stack([a["L3_xattn_bv"], a["L3_xattn_bo"], a["L3_xattn_ln_gamma"], a["L3_xattn_ln_beta"]])
    out["l3_mask"] = a["mask_BxS2_ik0"].T
    out["l3_rs"] = a["L3_xattn_residual_scale"].reshape(1)
    shared = lambda w: w.reshape(D, L3_SI // L3_I, L3_I).transpose(1, 0, 2)
    out["l3f_gate"] = np.concatenate([a["L3_ffn_w_gate"], shared(a["L3_ffn_shw_gate"])])
    out["l3f_up"] = np.concatenate([a["L3_ffn_w_up"], shared(a["L3_ffn_shw_up"])])
    out["l3f_down"] = np.concatenate([a["L3_ffn_w_down"], a["L3_ffn_shw_down"].reshape(L3_SI // L3_I, L3_I, D)])
    out["l3f_router"] = np.concatenate([a["L3_ffn_gate_w"], a["L3_ffn_shgate_w"][None]]).T


SUBLAYERS = [l0_attention, l0_ffn, l1_attention, l1_ffn, l2_attention, l2_ffn, l3_attention, l3_ffn]


class Tensors:
    pass


ARENA = 42160


def build(nc, dram, out):
    T = Tensors()
    T.dram = dram
    with ExitStack() as ctx:
        def sb(name, shape, dt=F32):
            return ctx.enter_context(nc.sbuf_tensor(name, shape, dt))

        def sem(name):
            return ctx.enter_context(nc.semaphore(name))

        T.X = sb("X", [P, B, D])
        T.XN = sb("XN", [P, B, D])
        T.XNT = sb("XNT", [P, DC, N])
        T.CTX = sb("CTX", [P, B, D])
        T.CTXT = sb("CTXT", [P, DC, N])
        T.ident = sb("ident", [P, P])
        T.ident16 = sb("ident16", [P, P], BF16)
        T.ones = sb("ones", [P, P])
        T.priority = sb("priority", [P, EXPERTS])
        T.bn = sb("bn", [P, B, 6])
        T.mv = sb("mv", [P, B, 2])
        T.vareps = sb("vareps", [P, B])
        T.rstd = sb("rstd", [P, B])
        T.minus_half = sb("minus_half", [P, 2 * P])
        arena = sb("arena", [P, ARENA])
        T.view = lambda at, n: arena[:, at:at + n]
        at = 24576
        T.Wh, T.DnT, T.wg, T.wo, T.gn, T.wfc, T.wproj = (
            T.view(at + a, n * k).rearrange("p (n k) -> p n k", n=n)
            for a, n, k in ((0, L0_H, L0_HD), (256, L0_H, S), (512, DC, D), (1024, DC, D), (1536, 2, D),
                            (2048, DC, L0_F), (4096, L0_FC, D)))
        T.wfc_in = sem("wfc_in")
        T.wproj_in = sem("wproj_in")
        T.PS = ctx.enter_context(nc.psum_tensor("PS", [P, BANKS, 512], F32))
        T.scratch = lambda name, shape, dt: nc.dram_tensor(name, shape, dt, kind="Internal").ap()
        more_tensors(T, sb, sem)

        consts_set, priority_in, stored = sem("consts_set"), sem("priority_in"), sem("stored")
        with nc.Block() as block:
            @block.sync
            def _(sp):
                sp.dma_start(T.priority[:, :], T.dram["priority"].unsqueeze(0).to_broadcast([P, EXPERTS])).then_inc(priority_in, 16)
                sp.wait_ge(priority_in, 16)

            @block.vector
            def _(dve):
                nc.vector.memset(T.ones[:, :], 1.0).then_inc(consts_set, 1)
                dve.wait_ge(consts_set, 1)
        for sublayer in SUBLAYERS:
            taken = []

            def own_sem(name):
                taken.append(nc.alloc_semaphore(name=name))
                return taken[-1]

            sublayer(nc, T, own_sem)
            nc.clear_and_free_semaphores(taken)
            nc.all_engine_barrier()
        with nc.Block() as block:
            @block.sync
            def _(sp):
                for b in range(0, B, 2):
                    sp.dma_start(out[b:b + 2].rearrange("b p d -> p b d"), T.X[:, b:b + 2, :]).then_inc(stored, 16)
                sp.wait_ge(stored, 16 * (B // 2))


def decay_masks():
    gam = (1.0 - 2.0 ** (-5.0 - np.arange(L0_H, dtype=np.float32))).astype(np.float32)
    idx = np.arange(S, dtype=np.float32)
    expo = idx[None, :] - idx[:, None]
    d = np.where(expo[None] <= 0, gam[:, None, None] ** np.minimum(expo, 0)[None], 0.0).astype(np.float32)
    d = d / np.sqrt(d.sum(axis=-1))[:, None, :]
    return np.ascontiguousarray((d / np.sqrt(np.float32(L0_HD))).transpose(0, 2, 1)).astype(np.float32)


def laid_out(inputs):
    a = {k: np.asarray(v) for k, v in inputs.items()}
    out = {
        "x": a["x"], "ctx": a["ctx_2048"], "ident": np.eye(P, dtype=np.float32), "dnT": decay_masks(),
        "Wh": a["L0_xattn_Wh"], "wg": a["L0_xattn_wg_w"], "wo": a["L0_xattn_wo_w"],
        "gn_gamma": a["L0_xattn_gn_gamma"], "gn_beta": a["L0_xattn_gn_beta"],
        "wfcT": a["L0_ffn_w_fc"].T, "wprojT": a["L0_ffn_w_proj"].T,
    }
    more_arrays(a, out)
    return {k: np.ascontiguousarray(v) for k, v in out.items()}


def kernel(**inputs):
    import concourse.bacc as bacc
    from concourse.bass_utils import run_bass_kernel_spmd

    nc = bacc.Bacc("TRN2", target_bir_lowering=False, num_devices=1)
    arrays = laid_out(inputs)
    dram = {k: nc.dram_tensor("in_" + k, v.shape, mybir.dt.from_np(v.dtype), kind="ExternalInput").ap()
            for k, v in arrays.items()}
    out = nc.dram_tensor("out_x", (B, S, D), F32, kind="ExternalOutput").ap()
    build(nc, dram, out)
    r = run_bass_kernel_spmd(nc, [{"in_" + k: v for k, v in arrays.items()}], core_ids=[0])
    return r.results[0]["out_x"]
```
